# Optimizing a Trainium2 kernel written in Bass

```python
import numpy as np
import jax
import jax.numpy as jnp

def _softmax(x, axis=-1):
    return jax.nn.softmax(x, axis=axis)

def _gelu(x):
    return jax.nn.gelu(x, approximate=True)

def _silu(x):
    return jax.nn.silu(x)

def _sigmoid(x):
    return jax.nn.sigmoid(x)

def _layernorm(x, axis=-1, eps=1e-05):
    m = jnp.mean(x, axis=axis, keepdims=True)
    v = jnp.var(x, axis=axis, keepdims=True)
    return (x - m) / jnp.sqrt(v + eps)

def _scatter_add(tgt, idx, src, axis=0):
    return tgt.at[idx].add(src)

def _segment_sum(src, seg, n):
    return jax.ops.segment_sum(src, seg, n)
kernel_name = 'mk_macaron_d1_jaxref_r8_aa1f4d'

def setup_inputs(seed: int=0):
    np.random.seed(seed)
    _w = jnp.asarray

    def _L0_attn_setup():
        import jax, jax.numpy as jnp
        import numpy as np
        D_MODEL = 256
        N_HEADS = 32
        HEAD_DIM = D_MODEL // N_HEADS
        B, T = (4, 512)

        def _reference_tuple_inner(x, W_in, W_out, log_A, W_dt, b_dt):
            Bsz, Tlen, D = x.shape
            H, hd = log_A.shape
            xp = jnp.einsum('btd,ed->bte', x, W_in)
            dt = jax.nn.softplus(jnp.einsum('btd,hd->bth', xp, W_dt) + b_dt)
            A_cont = -jnp.exp(log_A)
            a = jnp.exp(dt[..., None] * A_cont)
            xh = xp.reshape(Bsz, Tlen, H, hd)

            def combine(c1, c2):
                a1, u1 = c1
                a2, u2 = c2
                return (a1 * a2, a2 * u1 + u2)
            _, ys = jax.lax.associative_scan(combine, (a, xh), axis=1)
            s = ys[:, -1]
            y = jnp.einsum('btd,ed->bte', ys.reshape(Bsz, Tlen, D), W_out)
            return (y, s)
        key = jax.random.key(seed)
        ks = jax.random.split(key, 6)
        return {'x': jax.random.normal(ks[0], (B, T, D_MODEL), dtype=jnp.float32), 'W_in': jax.random.normal(ks[1], (D_MODEL, D_MODEL), dtype=jnp.float32) * (1.0 / np.sqrt(D_MODEL)), 'W_out': jax.random.normal(ks[2], (D_MODEL, D_MODEL), dtype=jnp.float32) * (1.0 / np.sqrt(D_MODEL)), 'log_A': jax.random.normal(ks[3], (N_HEADS, HEAD_DIM), dtype=jnp.float32) * 0.02, 'W_dt': jax.random.normal(ks[4], (N_HEADS, D_MODEL), dtype=jnp.float32) * (1.0 / np.sqrt(D_MODEL)), 'b_dt': jax.random.normal(ks[5], (N_HEADS,), dtype=jnp.float32) * 0.02}
    _L0_attn_in = _L0_attn_setup()

    def _L0_ffn_setup():
        import jax, jax.numpy as jnp
        import numpy as np
        TOP_K = 4
        key = jax.random.key(seed)
        ks = jax.random.split(key, 9)
        B, T, D, H, NE = (2, 128, 256, 176, 16)
        s = 0.02
        return {'x': jax.random.normal(ks[0], (B, T, D), jnp.float32), 'gate_w': jax.random.normal(ks[1], (NE, D), jnp.float32) * s, 'gate_b': jax.random.normal(ks[2], (NE,), jnp.float32) * s, 'w1_shared': jax.random.normal(ks[3], (D, H), jnp.float32) * s, 'w2_shared': jax.random.normal(ks[4], (H, D), jnp.float32) * s, 'w3_shared': jax.random.normal(ks[5], (D, H), jnp.float32) * s, 'w1_routed': jax.random.normal(ks[6], (NE, D, H), jnp.float32) * s, 'w2_routed': jax.random.normal(ks[7], (NE, H, D), jnp.float32) * s, 'w3_routed': jax.random.normal(ks[8], (NE, D, H), jnp.float32) * s}
    _L0_ffn_in = _L0_ffn_setup()
    _d = {'L0_attn_x': _L0_attn_in['x'], 'L0_attn_W_in': _L0_attn_in['W_in'], 'L0_attn_W_out': _L0_attn_in['W_out'], 'L0_attn_log_A': _L0_attn_in['log_A'], 'L0_attn_W_dt': _L0_attn_in['W_dt'], 'L0_attn_b_dt': _L0_attn_in['b_dt'], 'L0_ffn_gate_w': _L0_ffn_in['gate_w'], 'L0_ffn_gate_b': _L0_ffn_in['gate_b'], 'L0_ffn_w1_shared': _L0_ffn_in['w1_shared'], 'L0_ffn_w2_shared': _L0_ffn_in['w2_shared'], 'L0_ffn_w3_shared': _L0_ffn_in['w3_shared'], 'L0_ffn_w1_routed': _L0_ffn_in['w1_routed'], 'L0_ffn_w2_routed': _L0_ffn_in['w2_routed'], 'L0_ffn_w3_routed': _L0_ffn_in['w3_routed']}
    _x0 = _d['L0_attn_x']
    _d['L0_attn_x'] = jax.random.normal(jax.random.fold_in(jax.random.key(seed), 1), (4, 512, 256), dtype=_x0.dtype)
    del _x0
    return _d

def reference(L0_attn_x, L0_attn_W_in, L0_attn_W_out, L0_attn_log_A, L0_attn_W_dt, L0_attn_b_dt, L0_ffn_gate_w, L0_ffn_gate_b, L0_ffn_w1_shared, L0_ffn_w2_shared, L0_ffn_w3_shared, L0_ffn_w1_routed, L0_ffn_w2_routed, L0_ffn_w3_routed):

    def _L0_attn_ref(x, W_in, W_out, log_A, W_dt, b_dt):
        import jax, jax.numpy as jnp
        import numpy as np
        D_MODEL = 256
        N_HEADS = 32
        HEAD_DIM = D_MODEL // N_HEADS
        B, T = (4, 512)

        def _reference_tuple_inner(x, W_in, W_out, log_A, W_dt, b_dt):
            Bsz, Tlen, D = x.shape
            H, hd = log_A.shape
            xp = jnp.einsum('btd,ed->bte', x, W_in)
            dt = jax.nn.softplus(jnp.einsum('btd,hd->bth', xp, W_dt) + b_dt)
            A_cont = -jnp.exp(log_A)
            a = jnp.exp(dt[..., None] * A_cont)
            xh = xp.reshape(Bsz, Tlen, H, hd)

            def combine(c1, c2):
                a1, u1 = c1
                a2, u2 = c2
                return (a1 * a2, a2 * u1 + u2)
            _, ys = jax.lax.associative_scan(combine, (a, xh), axis=1)
            s = ys[:, -1]
            y = jnp.einsum('btd,ed->bte', ys.reshape(Bsz, Tlen, D), W_out)
            return (y, s)
        return _reference_tuple_inner(x, W_in, W_out, log_A, W_dt, b_dt)[0]

    def _L0_ffn_ref(x, gate_w, gate_b, w1_shared, w2_shared, w3_shared, w1_routed, w2_routed, w3_routed):
        import jax, jax.numpy as jnp
        import numpy as np
        TOP_K = 4
        n_experts = w1_routed.shape[0]
        logits = jnp.einsum('ed,btd->bte', gate_w, x)
        scores = jax.nn.sigmoid(logits) + gate_b
        weights, indices = jax.lax.top_k(scores, TOP_K)
        weights = weights / weights.sum(-1, keepdims=True)
        shared_out = jax.nn.silu(x @ w1_shared) * (x @ w3_shared) @ w2_shared
        one_hot = jax.nn.one_hot(indices, n_experts, dtype=x.dtype)
        router_probs = (weights[..., None] * one_hot).sum(-2)
        h1 = jnp.einsum('btd,edc->btec', x, w1_routed)
        h2 = jnp.einsum('btd,edc->btec', x, w3_routed)
        h3 = jax.nn.silu(h1 * h2)
        experts_out = jnp.einsum('btec,ecd->bted', h3, w2_routed)
        routed_out = jnp.einsum('bted,bte->btd', experts_out, router_probs)
        return shared_out + routed_out
    x = L0_attn_x
    x = x + 0.5 * _L0_ffn_ref(_layernorm(x, axis=-1), L0_ffn_gate_w, L0_ffn_gate_b, L0_ffn_w1_shared, L0_ffn_w2_shared, L0_ffn_w3_shared, L0_ffn_w1_routed, L0_ffn_w2_routed, L0_ffn_w3_routed)
    x = x + _L0_attn_ref(_layernorm(x, axis=-1), L0_attn_W_in, L0_attn_W_out, L0_attn_log_A, L0_attn_W_dt, L0_attn_b_dt)
    x = x + 0.5 * _L0_ffn_ref(_layernorm(x, axis=-1), L0_ffn_gate_w, L0_ffn_gate_b, L0_ffn_w1_shared, L0_ffn_w2_shared, L0_ffn_w3_shared, L0_ffn_w1_routed, L0_ffn_w2_routed, L0_ffn_w3_routed)
    return x

_drawn_inputs = setup_inputs


def setup_inputs(seed=0):
    import zlib

    import numpy as np

    out = dict(_drawn_inputs(seed))
    spreads = {}
    factors = {'L0_attn_log_A': 8.0,
     'L0_attn_b_dt': 8.0,
     'L0_ffn_gate_w': 8.0,
     'L0_ffn_gate_b': 8.0,
     'L0_ffn_w1_shared': 6.333,
     'L0_ffn_w2_shared': 6.248,
     'L0_ffn_w3_shared': 6.244,
     'L0_ffn_w1_routed': 8.0,
     'L0_ffn_w2_routed': 8.0,
     'L0_ffn_w3_routed': 8.0}
    for name, (base, spread) in spreads.items():
        noise = np.random.default_rng([zlib.crc32(name.encode()), seed]).standard_normal(out[name].shape)
        drawn = base * np.exp(spread * noise) if base else spread * noise
        out[name] = jnp.asarray(drawn.astype(out[name].dtype))
    for name, factor in factors.items():
        out[name] = (out[name] * factor).astype(out[name].dtype)
    return out
```

```python
import concourse.bass as bass
from concourse import mybir
from contextlib import ExitStack
import numpy as np

B, T, D = 4, 512, 256
H = 176
NE, TOPK = 16, 4
HEADS = 32
P = 128
N = B * T
NT = N // P
DC = D // P
HC = H // 2
NSLOT_MAX = (N * TOPK + NE * (P - 1)) // P
UN = 4
NS = -(-NSLOT_MAX // UN) * UN
STEPS = NT + NS
EPS = 1e-5
W13 = DC * 2 * H
W2C = 2 * D
WE = W13 + W2C
GS = 2 * H + NE
WSH = DC * GS + W2C
MCH = 256
NMC = N // MCH
MT = MCH // P
MAMBA_E = 12
MW = 3 * DC * D

C_ID, C_TOK, C_IE, C_J128, C_ONE, C_GB, C_MB = 0, 128, 144, 160, 176, 177, 193
NCST = C_MB + 4
H_TRI, H_ONE, H_I128, H_INS = 0, 128, 256, 384
NHCST = 384 + NS


def build(nc, x_d, w13r_d, w2r_d, w13s_d, w2s_d, wm_d, cst_d, hcst_d, out_d):
    f32, f32r, f16, i32, u32 = (mybir.dt.float32, mybir.dt.float32r, mybir.dt.float16,
                                mybir.dt.int32, mybir.dt.uint32)
    ALU = mybir.AluOpType
    ACT = mybir.ActivationFunctionType
    AX = mybir.AxisListType
    ds = bass.ds
    ctx = ExitStack()
    with ctx:
        def sb(name, shape, dt=f32):
            return ctx.enter_context(nc.sbuf_tensor(name, shape, dt))

        def sem(name):
            return ctx.enter_context(nc.semaphore(name))

        xn_dram = nc.dram_tensor("xn_scratch", (N, D), f32, kind="Internal").ap()
        ys_dram = nc.dram_tensor("ys_scratch", (NS * P, D), f32, kind="Internal").ap()

        w_routed = sb("w_routed", [P, NE, 2, WE], f32r)
        w_shared = sb("w_shared", [P, 2, WSH], f32r)
        stage = [sb("stage0", [P, WSH]), sb("stage1", [P, WE])]
        xres = sb("xres", [P, NT, D])
        ring_r = sb("ring_r", [P, 2048], f32r)
        ring_f = sb("ring_f", [P, 2048])
        xT = [[ring_r[:, (b * 2 + h) * 256:(b * 2 + h + 1) * 256] for h in range(2)] for b in range(2)]
        hT = [[ring_r[:, 1024 + (b * 2 + h) * 256:1024 + (b * 2 + h + 1) * 256] for h in range(2)] for b in range(2)]
        xg = [ring_f[:, k * D:(k + 1) * D] for k in range(UN)]
        hid = [ring_f[:, 1024 + b * H:1024 + (b + 1) * H] for b in range(2)]
        yb = [ring_f[:, 1376 + b * D:1376 + (b + 1) * D] for b in range(2)]
        oh = ring_f[:, 0:1024].rearrange("p (t k e) -> p t k e", t=NT, k=TOPK)
        prod = ring_f[:, 1024:2048].rearrange("p (t k e) -> p t k e", t=NT, k=TOPK)
        ring_h = ring_f[:, :].bitcast(f16)
        pickA = [ring_h[:, b * 512:(b + 1) * 512].rearrange("p (k s) -> p k s", k=TOPK) for b in range(2)]
        pickB = [ring_h[:, 1024 + b * TOPK * NS:1024 + (b + 1) * TOPK * NS].rearrange("p (k s) -> p k s", k=TOPK)
                 for b in range(2)]
        teq = ring_f[0:1, 0:NS * NE].rearrange("p (j e) -> p j e", e=NE)
        cg = [ring_f[:, b * 1024:(b + 1) * 1024].rearrange("p (k d) -> p k d", k=TOPK) for b in range(2)]
        cst = sb("cst", [P, NCST])
        hcst = sb("hcst", [P, NHCST], f16)
        ident = cst[:, C_ID:C_ID + P]
        stats = ring_f[:, 0:NT * 6].rearrange("p (t s) -> p t s", s=6)
        mv = ring_f[:, NT * 6:NT * 8].rearrange("p (t s) -> p t s", s=2)
        rstd = sb("rstd", [P, NT])
        nmr = sb("nmr", [P, NT])
        rt = [stage[0], stage[1]]
        lg = sb("lg", [P, NT, NE])
        si = sb("si", [P, NT * TOPK], i32)
        wk = sb("wk", [P, NT * TOPK])
        te = sb("te", [1, NS], i32)
        tokidx = sb("tokidx", [P, NS], i32)
        nega = sb("nega", [P, DC])
        ylast = sb("ylast", [P, DC])
        r0 = lambda a, b: rt[0][:, a:b]
        r1 = lambda a, b: rt[1][:, a:b]
        v8 = r0(0, 128).rearrange("p (t k) -> p t k", k=8)
        i8 = r0(128, 256).bitcast(u32).rearrange("p (t k) -> p t k", k=8)
        if4 = r0(256, 320)
        wsum = r0(320, 336)
        rw = r0(336, 352)
        slotf = r0(352, 416)
        loi = r0(416, 480).bitcast(i32)
        hii = r0(480, 544).bitcast(i32)
        lof = r0(544, 608)
        hif = r0(608, 672)
        memh = r0(672, 800).bitcast(f16)
        totT = r0(800, 1056)
        gsum = r1(0, 256)
        gexc = r1(256, 512)
        slot = r1(512, 768)
        cmpj = r1(768, 1024)
        cnt = r1(1024, 1040)
        ntl = r1(1040, 1056)
        ctl = r1(1056, 1072)
        tbx = r1(1072, 1088)
        off = r1(1088, 1104)
        tef = r1(1104, 1104 + NS)

        mroom = w_routed[:, MAMBA_E:NE, :, :].rearrange("p e h w -> p (e h w)")
        m_w = [mroom[:, h * MW:(h + 1) * MW] for h in range(2)]
        mo = 2 * MW
        m_xT = [mroom[:, mo + h * 512:mo + (h + 1) * 512] for h in range(2)]
        m_xp = [mroom[:, mo + 1024 + h * 512:mo + 1024 + (h + 1) * 512] for h in range(2)]
        m_ys = [mroom[:, mo + 2048 + h * 512:mo + 2048 + (h + 1) * 512] for h in range(2)]
        m_xn = ring_f[:, 0:512].rearrange("p (t d) -> p t d", t=MT)
        m_t = ring_f[:, 512:1024]
        m_r = ring_f[:, 1024:1536]
        m_y = ring_f[:, 1536:2048]

        pb = [ctx.enter_context(nc.psum_tensor(f"bank{i}", [P, 512], f32)) for i in range(8)]
        p_xT, p_h, p_hT, p_y = pb[0:2], pb[2:4], pb[4:6], pb[6:8]

        s_cst = sem("constants_loaded")
        s_x = [sem(f"x_loaded{i}") for i in range(4)]
        s_stg = [sem(f"stage_loaded{i}") for i in range(2)]
        s_whi = sem("weights_high")
        s_wlo = sem("weights_low")
        s_ln = sem("variances_ready")
        s_sd = sem("deviation_ready")
        s_xn = sem("xn_ready")
        s_xw = [sem(f"xn_written{k}") for k in range(UN)]
        s_g = [sem(f"gathered{k}") for k in range(UN)]
        s_xt = sem("x_transposed")
        s_xhi = sem("xT_high")
        s_xlo = sem("xT_low")
        s_h = sem("hidden_sums")
        s_lg = sem("logits_copied")
        s_a = sem("hidden_first")
        s_m = sem("hidden_product")
        s_s = sem("hidden_silu")
        s_ht = sem("hidden_transposed")
        s_hhi = sem("hT_high")
        s_hlo = sem("hT_low")
        s_y = sem("y_sums")
        s_yo = sem("y_out")
        s_yw = [sem(f"y_written{b}") for b in range(2)]
        s_sig = sem("sigmoid_ready")
        s_mem = sem("members_ready")
        s_cum = sem("counts_ready")
        s_pk = sem("picks_ready")
        s_pkd = sem("picks_used")
        s_rt = sem("routing_ready")
        s_cg = [sem(f"combine_gathered{b}") for b in range(2)]
        s_cd = sem("combined")
        s_dv = sem("dve_chain")
        s_fin = sem("layer_done")
        s_out = sem("out_written")
        m_s = {n: sem("m_" + n) for n in ("xn", "xt", "xhi", "xlo", "xp", "phi", "plo", "z", "abs", "relu", "ln",
                                          "sp", "a", "scan", "last", "yhi", "ylo", "y", "res", "neg")}

        block = ctx.enter_context(nc.Block())

        def item_parts(i, e=None):
            if i == "shared":
                return [(P, slice(0, DC * GS), lambda h: w_shared[:, h, 0:DC * GS]),
                        (HC, slice(DC * GS, WSH), lambda h: w_shared[0:HC, h, DC * GS:WSH])]
            if i == "routed":
                return [(P, slice(0, W13), lambda h: w_routed[:, ds(e, 1), h, 0:W13]),
                        (HC, slice(W13, WE), lambda h: w_routed[0:HC, ds(e, 1), h, W13:WE])]
            if i == "m1":
                return [(P, slice(0, 1024), lambda h: m_w[h][:, 0:1024])]
            return [(P, slice(0, 512), lambda h: m_w[h][:, 1024:MW])]

        ITEM_M = 17
        ITEM_AGAIN = 19

        @block.sync
        def _(sp):
            sp.dma_start(cst[:, :], cst_d).then_inc(s_cst, 16)
            x_v = x_d.rearrange("(t p) d -> p t d", p=P)
            for q in range(4):
                sp.dma_start(xres[:, 4 * q:4 * q + 4, :], x_v[:, 4 * q:4 * q + 4, :]).then_inc(s_x[q], 16)

            def load(b, wait, a_src, a_cols, b_src=None, b_cols=None):
                if wait is not None:
                    sp.wait_ge(s_wlo, wait)
                sp.dma_start(stage[b][:, 0:a_cols], a_src).then_inc(s_stg[b], 16)
                if b_src is not None:
                    sp.dma_start(stage[b][0:HC, a_cols:b_cols], b_src).then_inc(s_stg[b], 16)

            def load_expert(b, wait, e):
                load(b, wait, w13r_d[ds(e, 1), :, :].rearrange("o p c -> (o p) c"), W13,
                     w2r_d[ds(e, 1), :, :].rearrange("o p c -> (o p) c"), WE)

            def xn_out(f, t, k):
                sp.wait_ge(s_xn, f * NT + t + 1)
                sp.dma_start(xn_dram[ds(t * P, P), :], xg[k]).then_inc(s_xw[k], 16)

            def y_out(f, j, b):
                sp.wait_ge(s_yo, f * STEPS + NT + j + 1)
                sp.dma_start(ys_dram[ds(j * P, P), :], yb[b]).then_inc(s_yw[b], 16)

            load(0, None, w13s_d, DC * GS, w2s_d, WSH)
            sp.dma_start(hcst[:, :], hcst_d).then_inc(s_cst, 16)
            load_expert(1, None, 0)
            for f in range(2):
                if f == 0:
                    for t in range(UN):
                        xn_out(f, t, t)
                        load_expert(t % 2, t + 1, t + 1)
                    with sp.Fori(1, NT // UN - 1) as i:
                        for k in range(UN):
                            t = i * UN + k
                            xn_out(f, t, k)
                            load_expert(k % 2, t + 1, t + 1)
                    for k in range(UN):
                        t = NT - UN + k
                        xn_out(f, t, k)
                        if t + 1 < NE:
                            load_expert(k % 2, t + 1, t + 1)
                else:
                    for t in range(2):
                        load_expert((ITEM_AGAIN + t) % 2, ITEM_AGAIN + t - 1, MAMBA_E + t)
                    for t in range(UN):
                        xn_out(f, t, t)
                        if t + 2 < NE - MAMBA_E:
                            load_expert((ITEM_AGAIN + t) % 2, ITEM_AGAIN + t + 1, MAMBA_E + t + 2)
                    with sp.Fori(1, NT // UN) as i:
                        for k in range(UN):
                            xn_out(f, i * UN + k, k)
                with sp.Fori(0, NS // UN) as i:
                    for k in range(UN):
                        y_out(f, i * UN + k, k % 2)
                if f == 0:
                    load(ITEM_M % 2, ITEM_M, wm_d[:, 0:1024], 1024)
                    load((ITEM_M + 1) % 2, ITEM_M, wm_d[:, 1024:MW], 512)
            o_v = out_d.rearrange("(t p) d -> p t d", p=P)
            with sp.Fori(0, NT) as t:
                sp.wait_ge(s_cd, TOPK * NT + TOPK * (t + 1))
                sp.dma_start(o_v[:, ds(t, 1), :], xres[:, ds(t, 1), :]).then_inc(s_out, 16)
            sp.wait_ge(s_out, 16 * NT)

        @block.gpsimd
        def _(pool):
            def low(parts, b):
                for n, (rows, cols, view) in enumerate(parts):
                    last = pool.tensor_tensor(view(1), stage[b][0:rows, cols], view(0).bitcast(f32), ALU.subtract)
                last.then_inc(s_wlo, 1)

            def low_item(i, kind, b, e=None):
                pool.wait_ge(s_whi, i + 1)
                low(item_parts(kind, e), b)

            def gather(f, j):
                if j >= UN:
                    pool.wait_ge(s_xt, f * STEPS + NT + j - UN + 1)
                pool.indirect_dma_start(xg[j % UN], None, xn_dram,
                                        bass.IndirectOffsetOnAxis(ap=tokidx[:, j:j + 1], axis=0)
                                        ).then_inc(s_g[j % UN], 16)

            def combine(f, t):
                if t >= 2:
                    pool.wait_ge(s_cd, TOPK * (f * NT + t - 1))
                for q in range(t * TOPK, (t + 1) * TOPK):
                    pool.indirect_dma_start(cg[t % 2][:, q % TOPK, :], None, ys_dram,
                                            bass.IndirectOffsetOnAxis(ap=si[:, q:q + 1], axis=0)
                                            ).then_inc(s_cg[t % 2], 16)

            low_item(0, "shared", 0)
            for f in range(2):
                if f == 0:
                    with pool.Fori(0, NT // UN) as i:
                        for k in range(UN):
                            low_item(i * UN + k + 1, "routed", (k + 1) % 2, i * UN + k)
                else:
                    for t in range(UN):
                        low_item(ITEM_AGAIN + t, "routed", (ITEM_AGAIN + t) % 2, MAMBA_E + t)
                pool.wait_ge(s_rt, f + 1)
                for k in range(UN):
                    pool.wait_ge(s_xw[k], 16 * (NT // UN) * (f + 1))
                for j in range(NS):
                    gather(f, j)
                for b in range(2):
                    pool.wait_ge(s_yw[b], 16 * (NS // 2) * (f + 1))
                for t in range(NT):
                    combine(f, t)
                if f == 0:
                    low_item(ITEM_M, "m1", ITEM_M % 2)
                    low_item(ITEM_M + 1, "m2", (ITEM_M + 1) % 2)

        @block.scalar
        def _(act):
            def high(parts, b):
                for rows, cols, view in parts:
                    last = act.activation(view(0), stage[b][0:rows, cols], ACT.Copy)
                last.then_inc(s_whi, 1)

            def high_item(b, uses, kind, dmas, e=None):
                act.wait_ge(s_stg[b], 16 * uses)
                high(item_parts(kind, e), b)

            def deviation(l):
                act.wait_ge(s_ln, l + 1)
                act.activation(rstd[:, :], rstd[:, :], ACT.Sqrt).then_inc(s_sd, 1)

            def x_high(n, b, first):
                act.wait_ge(s_xt, n + 1)
                if not first:
                    act.wait_ge(s_h, n - 1)
                act.activation(xT[b][0], p_xT[b][:, 0:DC * P], ACT.Copy).then_inc(s_xhi, 1)

            def h_high(n, b, first):
                act.wait_ge(s_ht, n + 1)
                if not first:
                    act.wait_ge(s_y, n - 1)
                act.activation(hT[b][0][0:HC, :], p_hT[b][0:HC, 0:2 * P], ACT.Copy).then_inc(s_hhi, 1)

            def shared_step(f, t, k, stages):
                n = f * STEPS + t
                b = k % 2
                if 1 in stages:
                    act.wait_ge(s_h, n)
                    act.activation(lg[:, ds(t - 1, 1), :], p_h[1 - b][:, 2 * H:GS], ACT.Copy).then_inc(s_lg, 1)
                    if not (f == 0 and isinstance(t, int) and t <= 2):
                        act.wait_ge(s_ht, n - 2)
                    act.activation(hid[1 - b], p_h[1 - b][:, 0:H], ACT.Silu).then_inc(s_a, 1)
                if 0 in stages:
                    x_high(n, b, f == 0 and isinstance(t, int) and t < 2)
                if 2 in stages:
                    h_high(n - 2, b, f == 0 and isinstance(t, int) and t < 4)

            def slot_step(f, j, k, stages):
                n = f * STEPS + NT + j
                b = k % 2
                if 1 in stages:
                    act.wait_ge(s_h, n)
                    act.wait_ge(s_ht, n - 2)
                    act.activation(hid[1 - b], p_h[1 - b][:, H:2 * H], ACT.Copy).then_inc(s_a, 1)
                if 0 in stages:
                    x_high(n, b, False)
                if 1 in stages:
                    act.wait_ge(s_m, n)
                    act.activation(hid[1 - b], hid[1 - b], ACT.Silu).then_inc(s_s, 1)
                if 2 in stages:
                    h_high(n - 2, b, False)

            act.wait_ge(s_cst, 16)
            high_item(0, 2, "shared", 2)
            deviation(0)
            for f in range(2):
                for t in range(UN):
                    shared_step(f, t, t, set(range(min(t, 2) + 1)))
                    if f == 0:
                        high_item((t + 1) % 2, 2 * ((t + 1) // 2 + 1), "routed", 2, t)
                    else:
                        b = (ITEM_AGAIN + t) % 2
                        high_item(b, M_BASE[b] + 2 * (t // 2 + 1), "routed", 2, MAMBA_E + t)
                with act.Fori(1, NT // UN) as i:
                    for k in range(UN):
                        t = i * UN + k
                        shared_step(f, t, k, {0, 1, 2})
                        if f == 0:
                            high_item((k + 1) % 2, (i * UN + 2 * ((k + 1) // 2)) + 2, "routed", 2, t)
                shared_step(f, NT, 0, {1, 2})
                shared_step(f, NT + 1, 1, {2})
                act.wait_ge(s_lg, NT * (f + 1))
                act.activation(lg[:, :, :], lg[:, :, :], ACT.Sigmoid).then_inc(s_sig, 1)
                slot_step(f, 0, 0, {0})
                slot_step(f, 1, 1, {0, 1})
                slot_step(f, 2, 2, {0, 1, 2})
                slot_step(f, 3, 3, {0, 1, 2})
                with act.Fori(1, NS // UN) as i:
                    for k in range(UN):
                        slot_step(f, i * UN + k, k, {0, 1, 2})
                slot_step(f, NS, 0, {1, 2})
                slot_step(f, NS + 1, 1, {2})
                if f == 0:
                    act.wait_ge(s_y, STEPS)
                    for q, kind in ((ITEM_M, "m1"), (ITEM_M + 1, "m2")):
                        high_item(q % 2, M_FIRST[q % 2] + 1, kind, 1)
                    deviation(1)
                    act.activation(nega[:, :], cst[:, C_MB:C_MB + DC], ACT.Exp).then_inc(m_s["neg"], 1)
                    act.wait_ge(m_s["neg"], 1)
                    act.activation(nega[:, :], nega[:, :], ACT.Copy, scale=-1.0).then_inc(m_s["neg"], 1)

                    def m_chunk(c, first):
                        act.wait_ge(m_s["xt"], c + 1)
                        act.activation(m_xT[0], pb[0][:, :], ACT.Copy).then_inc(m_s["xhi"], 1)
                        act.wait_ge(m_s["xp"], c + 1)
                        act.activation(m_xp[0], pb[1][:, :], ACT.Copy).then_inc(m_s["phi"], 1)
                        act.wait_ge(m_s["z"], c + 1)
                        if not first:
                            act.wait_ge(m_s["scan"], c)
                        for q in range(DC):
                            last = act.activation(m_t[:, q * MCH:(q + 1) * MCH], pb[2][:, q * MCH:(q + 1) * MCH],
                                                  ACT.Abs, bias=cst[:, C_MB + DC + q:C_MB + DC + q + 1])
                        last.then_inc(m_s["abs"], 1)
                        act.wait_ge(m_s["abs"], 3 * c + 1)
                        act.activation(m_t, m_t, ACT.Exp, scale=-1.0).then_inc(m_s["abs"], 1)
                        act.wait_ge(m_s["abs"], 3 * c + 2)
                        act.activation(m_t, m_t, ACT.Ln, bias=1.0).then_inc(m_s["abs"], 1)
                        act.wait_ge(m_s["sp"], c + 1)
                        for q in range(DC):
                            last = act.activation(m_t[:, q * MCH:(q + 1) * MCH], m_t[:, q * MCH:(q + 1) * MCH],
                                                  ACT.Exp, scale=nega[:, q:q + 1])
                        last.then_inc(m_s["a"], 1)
                        act.wait_ge(m_s["scan"], c + 1)
                        act.activation(m_ys[0], m_y, ACT.Copy).then_inc(m_s["yhi"], 1)

                    act.wait_ge(m_s["neg"], 2)
                    m_chunk(0, True)
                    with act.Fori(1, NMC) as c:
                        m_chunk(c, False)
                    deviation(2)

        @block.vector
        def _(dve):
            chain = [0]

            def link(ins):
                chain[0] += 1
                ins.then_inc(s_dv, 1)
                dve.wait_ge(s_dv, chain[0])

            def variances():
                for t in range(NT):
                    last = dve.bn_stats(stats[:, t, :], xres[:, t, :])
                link(last)
                for t in range(NT):
                    last = dve.bn_aggr(mv[:, t, :], stats[:, t, :])
                link(last)
                dve.tensor_scalar(rstd[:, :], mv[:, :, 1], EPS, None, ALU.add).then_inc(s_ln, 1)

            def scales(l):
                dve.wait_ge(s_sd, l + 1)
                link(dve.reciprocal(rstd[:, :], rstd[:, :]))
                link(dve.scalar_tensor_tensor(nmr[:, :], mv[:, :, 0], -1.0, rstd[:, :], ALU.mult, ALU.mult))

            def norm(f, i, k, first):
                t = i * UN + k
                if not first:
                    dve.wait_ge(s_xt, f * STEPS + t - UN + 1)
                    dve.wait_ge(s_xw[k], (f * (NT // UN) + i) * 16)
                dve.tensor_scalar(xg[k], xres[:, ds(t, 1), :].rearrange("p o d -> p (o d)"), rstd[:, ds(t, 1)],
                                  nmr[:, ds(t, 1)], ALU.mult, ALU.add).then_inc(s_xn, 1)

            def x_low(n, b):
                dve.wait_ge(s_xhi, n + 1)
                dve.tensor_tensor(xT[b][1], p_xT[b][:, 0:DC * P], xT[b][0].bitcast(f32),
                                  ALU.subtract).then_inc(s_xlo, 1)

            def h_low(n, b):
                dve.wait_ge(s_hhi, n + 1)
                dve.tensor_tensor(hT[b][1][0:HC, :], p_hT[b][0:HC, 0:2 * P], hT[b][0][0:HC, :].bitcast(f32),
                                  ALU.subtract).then_inc(s_hlo, 1)

            def shared_step(f, t, k, stages):
                n = f * STEPS + t
                b = k % 2
                if 1 in stages:
                    dve.wait_ge(s_a, n)
                    dve.tensor_tensor(hid[1 - b], p_h[1 - b][:, H:2 * H], hid[1 - b], ALU.mult).then_inc(s_m, 1)
                if 0 in stages:
                    x_low(n, b)
                if 3 in stages:
                    dve.wait_ge(s_y, n - 2)
                    xr = xres[:, ds(t - 3, 1), :].rearrange("p o d -> p (o d)")
                    dve.scalar_tensor_tensor(xr, p_y[1 - b][:, 0:D], 0.5, xr, ALU.mult, ALU.add).then_inc(s_yo, 1)
                if 2 in stages:
                    h_low(n - 2, b)

            def slot_step(f, i, k, stages, first=False):
                j = i * UN + k
                n = f * STEPS + NT + j
                b = k % 2
                if 1 in stages:
                    dve.wait_ge(s_a, n)
                    dve.tensor_tensor(hid[1 - b], p_h[1 - b][:, 0:H], hid[1 - b], ALU.mult).then_inc(s_m, 1)
                if 0 in stages:
                    x_low(n, b)
                if 3 in stages:
                    dve.wait_ge(s_y, n - 2)
                    if not first:
                        dve.wait_ge(s_yw[1 - b], 16 * (f * (NS // 2) + i * (UN // 2) + (k - 5) // 2 + 1))
                    dve.tensor_copy(yb[1 - b], p_y[1 - b][:, 0:D]).then_inc(s_yo, 1)
                if 2 in stages:
                    h_low(n - 2, b)

            def route(f):
                dve.wait_ge(s_sig, f + 1)
                dve.wait_ge(s_wlo, ITEM_M if f == 0 else ITEM_AGAIN + UN)
                link(dve.tensor_tensor(lg[:, :, :], lg[:, :, :],
                                       cst[:, C_GB:C_GB + NE].unsqueeze(1).broadcast_to((P, NT, NE)), ALU.add))
                for t in range(NT):
                    last = dve.max(v8[:, t, :], lg[:, t, :])
                link(last)
                for t in range(NT):
                    last = dve.max_index(i8[:, t, :], v8[:, t, :], lg[:, t, :])
                link(last)
                v4 = v8[:, :, 0:TOPK]
                if4v = if4.rearrange("p (t k) -> p t k", k=TOPK)
                link(dve.tensor_copy(if4v, i8[:, :, 0:TOPK]))
                for k in range(UN):
                    dve.wait_ge(s_xw[k], 16 * (NT // UN) * (f + 1))
                ie = cst[:, C_IE:C_IE + NE]
                link(dve.tensor_tensor(oh.rearrange("p t k e -> p (t k) e"),
                                       if4.unsqueeze(2).broadcast_to((P, NT * TOPK, NE)),
                                       ie.unsqueeze(1).broadcast_to((P, NT * TOPK, NE)), ALU.is_equal))
                dve.tensor_reduce(prod.rearrange("p t k e -> p (t k e)")[:, 0:NT * NE].rearrange(
                    "p (t e) -> p t e", e=NE), oh.rearrange("p t k e -> p t e k"), AX.X, ALU.add
                    ).then_inc(s_dv, 1)
                chain[0] += 1
                dve.wait_ge(s_dv, chain[0])
                dve.tensor_copy(memh, prod.rearrange("p t k e -> p (t k e)")[:, 0:NT * NE]).then_inc(s_mem, 1)
                link(dve.tensor_reduce(wsum, v4, AX.X, ALU.add))
                link(dve.reciprocal(rw, wsum))
                link(dve.tensor_scalar(rw, rw, 0.5, None, ALU.mult))
                link(dve.tensor_tensor(wk[:, :].rearrange("p (t k) -> p t k", k=TOPK), v4,
                                       rw.unsqueeze(2).broadcast_to((P, NT, TOPK)), ALU.mult))
                dve.wait_ge(s_cum, f + 1)
                totTv = totT.rearrange("p (e t) -> p e t", e=NE)
                link(dve.tensor_copy(totTv, pb[1][:, 0:NT * NE].rearrange("p (t e) -> p e t", e=NE)))
                one = cst[:, C_ONE:C_ONE + 1]
                link(dve.tensor_tensor_scan(gsum, one.broadcast_to((P, NT * NE)), totT, 0.0, ALU.mult, ALU.add))
                link(dve.tensor_tensor(gexc, gsum, totT, ALU.subtract))
                gs3 = gsum.rearrange("p (e t) -> p e t", e=NE)
                ge3 = gexc.rearrange("p (e t) -> p e t", e=NE)
                link(dve.tensor_tensor(cnt, gs3[:, :, NT - 1], ge3[:, :, 0], ALU.subtract))
                cj = cmpj.rearrange("p (e j) -> p e j", e=NE)
                link(dve.tensor_tensor(cj, cnt.unsqueeze(2).broadcast_to((P, NE, 16)),
                                       cst[:, C_J128:C_J128 + 16].unsqueeze(1).broadcast_to((P, NE, 16)), ALU.is_gt))
                link(dve.tensor_reduce(ntl, cj, AX.X, ALU.add))
                link(dve.tensor_tensor_scan(ctl, one.broadcast_to((P, NE)), ntl, 0.0, ALU.mult, ALU.add))
                link(dve.tensor_tensor(tbx, ctl, ntl, ALU.subtract))
                link(dve.scalar_tensor_tensor(off, tbx, float(P), ge3[:, :, 0], ALU.mult, ALU.subtract))
                sl = slot.rearrange("p (t e) -> p t e", e=NE)
                link(dve.tensor_tensor(sl, pb[0][:, 0:NT * NE].rearrange("p (t e) -> p t e", e=NE),
                                       gexc.rearrange("p (e t) -> p t e", e=NE), ALU.add))
                link(dve.tensor_tensor(sl, sl, off.unsqueeze(1).broadcast_to((P, NT, NE)), ALU.add))
                for k in range(TOPK):
                    last = dve.tensor_tensor(prod[:, :, k, :], oh[:, :, k, :], sl, ALU.mult)
                link(last)
                link(dve.tensor_reduce(slotf, prod.rearrange("p t k e -> p (t k) e"), AX.X, ALU.add))
                link(dve.tensor_copy(si[:, :], slotf))
                dve.tensor_single_scalar(loi, si[:, :], P - 1, ALU.bitwise_and)
                link(dve.tensor_single_scalar(hii, si[:, :], 7, ALU.logical_shift_right))
                dve.tensor_copy(lof, loi)
                link(dve.tensor_copy(hif, hii))
                for t in range(NT):
                    if t >= 2:
                        dve.wait_ge(s_pkd, f * NT + t - 1)
                    for k in range(TOPK):
                        q = t * TOPK + k
                        dve.tensor_scalar(pickA[t % 2][:, k, :], hcst[:, H_I128:H_I128 + P], lof[:, q:q + 1],
                                          cst[:, C_TOK + t:C_TOK + t + 1], ALU.is_equal, ALU.mult)
                        last = dve.tensor_scalar(pickB[t % 2][:, k, :], hcst[:, H_INS:H_INS + NS], hif[:, q:q + 1],
                                                 None, ALU.is_equal)
                    last.then_inc(s_pk, 1)
                dve.wait_ge(s_pkd, (f + 1) * NT)
                link(dve.tensor_tensor(teq, hcst[0:1, H_INS:H_INS + NS].unsqueeze(2).broadcast_to((1, NS, NE)),
                                       ctl[0:1, :].unsqueeze(1).broadcast_to((1, NS, NE)), ALU.is_ge))
                link(dve.tensor_reduce(tef[0:1, :], teq, AX.X, ALU.add))
                link(dve.tensor_scalar(te[:, :], tef[0:1, :], float(NE - 1), None, ALU.min))
                dve.tensor_copy(tokidx[:, :], pb[2][:, 0:NS]).then_inc(s_rt, 1)

            def combine(f, i, b):
                t = i * 2 + b
                dve.wait_ge(s_cg[b], 16 * TOPK * (f * (NT // 2) + i + 1))
                xr = xres[:, ds(t, 1), :].rearrange("p o d -> p (o d)")
                for q in range(TOPK):
                    dve.scalar_tensor_tensor(xr, cg[b][:, q, :], wk[:, ds(t * TOPK + q, 1)], xr,
                                             ALU.mult, ALU.add).then_inc(s_cd, 1)
                    dve.wait_ge(s_cd, TOPK * (f * NT + t) + q + 1)

            for q in range(4):
                dve.wait_ge(s_x[q], 16)
            dve.wait_ge(s_cst, 32)
            variances()
            scales(0)
            for f in range(2):
                for k in range(UN):
                    norm(f, 0, k, f == 0)
                    shared_step(f, k, k, {0} | ({1} if k >= 1 else set()) | ({2} if k >= 2 else set())
                                | ({3} if k >= 3 else set()))
                with dve.Fori(1, NT // UN) as i:
                    for k in range(UN):
                        norm(f, i, k, False)
                        shared_step(f, i * UN + k, k, {0, 1, 2, 3})
                shared_step(f, NT, 0, {1, 2, 3})
                shared_step(f, NT + 1, 1, {2, 3})
                shared_step(f, NT + 2, 2, {3})
                route(f)
                slot_step(f, 0, 0, {0})
                slot_step(f, 0, 1, {0, 1})
                slot_step(f, 0, 2, {0, 1, 2})
                slot_step(f, 0, 3, {0, 1, 2, 3}, True)
                slot_step(f, 1, 0, {0, 1, 2, 3}, True)
                for k in range(1, UN):
                    slot_step(f, 1, k, {0, 1, 2, 3})
                with dve.Fori(2, NS // UN) as i:
                    for k in range(UN):
                        slot_step(f, i, k, {0, 1, 2, 3})
                slot_step(f, NS // UN, 0, {1, 2, 3})
                slot_step(f, NS // UN, 1, {2, 3})
                slot_step(f, NS // UN, 2, {3})
                with dve.Fori(0, NT // 2) as i:
                    for b in range(2):
                        combine(f, i, b)
                if f == 0:
                    variances()
                    scales(1)

                    def m_chunk(c, b, first):
                        if not first:
                            dve.wait_ge(m_s["xt"], c)
                        for q in range(MT):
                            t = c * MT + q
                            last = dve.tensor_scalar(m_xn[:, q, :], xres[:, ds(t, 1), :].rearrange("p o d -> p (o d)"),
                                                     rstd[:, ds(t, 1)], nmr[:, ds(t, 1)], ALU.mult, ALU.add)
                        last.then_inc(m_s["xn"], 1)
                        dve.wait_ge(m_s["xhi"], c + 1)
                        dve.tensor_tensor(m_xT[1], pb[0][:, :], m_xT[0].bitcast(f32), ALU.subtract
                                          ).then_inc(m_s["xlo"], 1)
                        dve.wait_ge(m_s["phi"], c + 1)
                        dve.tensor_tensor(m_xp[1], pb[1][:, :], m_xp[0].bitcast(f32), ALU.subtract
                                          ).then_inc(m_s["plo"], 1)
                        dve.wait_ge(m_s["abs"], 3 * c + 1)
                        for q in range(DC):
                            last = dve.tensor_scalar(m_r[:, q * MCH:(q + 1) * MCH], pb[2][:, q * MCH:(q + 1) * MCH],
                                                     cst[:, C_MB + DC + q:C_MB + DC + q + 1], 0.0, ALU.add, ALU.max)
                        last.then_inc(m_s["relu"], 1)
                        dve.wait_ge(m_s["relu"], c + 1)
                        dve.wait_ge(m_s["abs"], 3 * c + 3)
                        dve.tensor_tensor(m_t, m_t, m_r, ALU.add).then_inc(m_s["sp"], 1)
                        dve.wait_ge(m_s["a"], c + 1)
                        if not first:
                            dve.wait_ge(m_s["ylo"], c)
                        for q in range(DC):
                            s = slice(q * MCH, (q + 1) * MCH)
                            last = dve.tensor_tensor_scan(m_y[:, s], m_t[:, s], pb[1][:, s],
                                                          0.0 if b == 0 else ylast[:, q:q + 1], ALU.mult, ALU.add)
                        last.then_inc(m_s["scan"], 1)
                        dve.wait_ge(m_s["scan"], c + 1)
                        dve.tensor_copy(ylast[:, :], m_y.rearrange("p (q s) -> p q s", q=DC)[:, :, MCH - 1]
                                        ).then_inc(m_s["last"], 1)
                        dve.wait_ge(m_s["last"], c + 1)
                        dve.wait_ge(m_s["yhi"], c + 1)
                        dve.tensor_tensor(m_ys[1], m_y, m_ys[0].bitcast(f32), ALU.subtract).then_inc(m_s["ylo"], 1)
                        dve.wait_ge(m_s["y"], c + 1)
                        xr = xres[:, ds(c * MT, MT), :]
                        dve.tensor_tensor(xr, xr, pb[3][:, :].rearrange("p (t d) -> p t d", t=MT), ALU.add
                                          ).then_inc(m_s["res"], 1)

                    m_chunk(0, 0, True)
                    m_chunk(1, 1, False)
                    with dve.Fori(1, NMC // 2) as i:
                        for b in range(2):
                            m_chunk(i * 2 + b, b, False)
                    dve.wait_ge(m_s["res"], NMC)
                    variances()
                    scales(2)

        @block.tensor
        def _(pe):
            def mm3(out, pairs):
                terms = [(a, b) for (a0, a1, b0, b1) in pairs for a, b in ((a0, b0), (a0, b1), (a1, b0))]
                for q, (a, b) in enumerate(terms):
                    last = pe.matmul(out, a, b, start=(q == 0), stop=(q == len(terms) - 1))
                return last

            def x_turn(n, b, k, first):
                if not first:
                    pe.wait_ge(s_xlo, n - 1)
                for c in range(DC):
                    last = pe.transpose(p_xT[b][:, c * P:(c + 1) * P], xg[k][:, c * P:(c + 1) * P], ident)
                last.then_inc(s_xt, 1)

            def h_turn(n, b, first):
                if not first:
                    pe.wait_ge(s_hlo, n - 1)
                for c in range(2):
                    last = pe.transpose(p_hT[b][0:HC, c * P:(c + 1) * P], hid[b][:, c * HC:(c + 1) * HC], ident)
                last.then_inc(s_ht, 1)

            def hidden(n, b, w, cols, chunk, first):
                pe.wait_ge(s_xlo, n + 1)
                if not first:
                    pe.wait_ge(s_m, n - 1)
                mm3(p_h[b][:, 0:cols], [(xT[b][0][:, c * P:(c + 1) * P], xT[b][1][:, c * P:(c + 1) * P],
                                         w(0, c * chunk, cols), w(1, c * chunk, cols)) for c in range(DC)]
                    ).then_inc(s_h, 1)

            def project(n, b, w, w0, first):
                pe.wait_ge(s_hlo, n + 1)
                if not first:
                    pe.wait_ge(s_yo, n - 1)
                mm3(p_y[b][:, 0:D], [(hT[b][0][0:HC, c * P:(c + 1) * P], hT[b][1][0:HC, c * P:(c + 1) * P],
                                      w(0, w0 + c * D, D), w(1, w0 + c * D, D)) for c in range(2)]
                    ).then_inc(s_y, 1)

            def shared_step(f, t, k, stages):
                n = f * STEPS + t
                b = k % 2
                early = f == 0 and isinstance(t, int)
                if 1 in stages:
                    hidden(n - 1, 1 - b, lambda h, c, m: w_shared[:, h, c:c + m], GS, GS, early and t - 1 < 2)
                if 0 in stages:
                    pe.wait_ge(s_xn, f * NT + t + 1)
                    x_turn(n, b, k, early and t < 2)
                if 3 in stages:
                    project(n - 3, 1 - b, lambda h, c, m: w_shared[0:HC, h, c:c + m], DC * GS, early and t - 3 < 2)
                if 2 in stages:
                    pe.wait_ge(s_m, n - 1)
                    h_turn(n - 2, b, early and t - 2 < 2)

            def slot_step(f, i, k, stages):
                j = i * UN + k
                n = f * STEPS + NT + j
                b = k % 2
                if 1 in stages:
                    e1 = pe.value_load(te[0:1, ds(j - 1, 1)], min_val=0, max_val=NE - 1)
                    hidden(n - 1, 1 - b, lambda h, c, m: w_routed[:, ds(e1, 1), h, c:c + m], 2 * H, 2 * H, False)
                if 0 in stages:
                    pe.wait_ge(s_g[k], 16 * (f * (NS // UN) + i + 1))
                    x_turn(n, b, k, False)
                if 3 in stages:
                    e3 = pe.value_load(te[0:1, ds(j - 3, 1)], min_val=0, max_val=NE - 1)
                    project(n - 3, 1 - b, lambda h, c, m: w_routed[0:HC, ds(e3, 1), h, c:c + m], W13, False)
                if 2 in stages:
                    pe.wait_ge(s_s, f * NS + j - 1)
                    h_turn(n - 2, b, False)

            pe.wait_ge(s_cst, 32)
            pe.wait_ge(s_wlo, 1)
            for f in range(2):
                for k in range(UN):
                    shared_step(f, k, k, set(range(k + 1)))
                with pe.Fori(1, NT // UN) as i:
                    for k in range(UN):
                        shared_step(f, i * UN + k, k, {0, 1, 2, 3})
                shared_step(f, NT, 0, {1, 2, 3})
                shared_step(f, NT + 1, 1, {2, 3})
                shared_step(f, NT + 2, 2, {3})
                pe.wait_ge(s_mem, f + 1)
                pe.matmul(pb[0][:, 0:NT * NE], hcst[:, H_TRI:H_TRI + P], memh, start=True, stop=True)
                pe.matmul(pb[1][:, 0:NT * NE], hcst[:, H_ONE:H_ONE + P], memh, start=True, stop=True
                          ).then_inc(s_cum, 1)
                for t in range(NT):
                    pe.wait_ge(s_pk, f * NT + t + 1)
                    for k in range(TOPK):
                        last = pe.matmul(pb[2][:, 0:NS], pickA[t % 2][:, k, :], pickB[t % 2][:, k, :],
                                         start=(t == 0 and k == 0), stop=(t == NT - 1 and k == TOPK - 1))
                    last.then_inc(s_pkd, 1)
                pe.wait_ge(s_rt, f + 1)
                pe.wait_ge(s_wlo, 17 if f == 0 else ITEM_AGAIN + UN)
                for k in range(UN):
                    slot_step(f, 0, k, set(range(k + 1)))
                with pe.Fori(1, NS // UN) as i:
                    for k in range(UN):
                        slot_step(f, i, k, {0, 1, 2, 3})
                slot_step(f, NS // UN, 0, {1, 2, 3})
                slot_step(f, NS // UN, 1, {2, 3})
                slot_step(f, NS // UN, 2, {3})
                if f == 0:
                    pe.wait_ge(s_wlo, ITEM_AGAIN)

                    def m_chunk(c, first):
                        wc = lambda h, m, q: m_w[h][:, (m * DC + q) * D:(m * DC + q + 1) * D]
                        pe.wait_ge(m_s["xn"], c + 1)
                        if not first:
                            pe.wait_ge(m_s["xlo"], c)
                        for q in range(DC):
                            for s in range(MT):
                                last = pe.transpose(pb[0][:, q * MCH + s * P:q * MCH + (s + 1) * P],
                                                    m_xn[:, s, q * P:(q + 1) * P], ident)
                        last.then_inc(m_s["xt"], 1)
                        for bank, m, src, ready, done in ((1, 0, m_xT, "xlo", "xp"), (2, 1, m_xp, "plo", "z")):
                            pe.wait_ge(m_s[ready], c + 1)
                            if not first:
                                pe.wait_ge(m_s["scan" if m == 0 else "relu"], c)
                            for e in range(DC):
                                last = mm3(pb[bank][:, e * MCH:(e + 1) * MCH],
                                           [(wc(0, m, q)[:, e * P:(e + 1) * P], wc(1, m, q)[:, e * P:(e + 1) * P],
                                             src[0][:, q * MCH:(q + 1) * MCH], src[1][:, q * MCH:(q + 1) * MCH])
                                            for q in range(DC)])
                            last.then_inc(m_s[done], 1)
                        pe.wait_ge(m_s["ylo"], c + 1)
                        if not first:
                            pe.wait_ge(m_s["res"], c)
                        for s in range(MT):
                            last = mm3(pb[3][:, s * D:(s + 1) * D],
                                       [(m_ys[0][:, q * MCH + s * P:q * MCH + (s + 1) * P],
                                         m_ys[1][:, q * MCH + s * P:q * MCH + (s + 1) * P],
                                         wc(0, 2, q), wc(1, 2, q)) for q in range(DC)])
                        last.then_inc(m_s["y"], 1)

                    m_chunk(0, True)
                    with pe.Fori(1, NMC) as c:
                        m_chunk(c, False)


M_FIRST = [18, 16]
M_BASE = [19, 17]


def _constants():
    c = np.zeros((P, NCST), np.float32)
    c[:, C_ID:C_ID + P] = np.eye(P)
    c[:, C_TOK:C_TOK + NT] = np.arange(NT)[None, :] * P + np.arange(P)[:, None]
    c[:, C_IE:C_IE + NE] = np.arange(NE)
    c[:, C_J128:C_J128 + 16] = np.arange(16) * P
    c[:, C_ONE] = 1.0
    h = np.zeros((P, NHCST), np.float16)
    h[:, H_TRI:H_TRI + P] = np.triu(np.ones((P, P)), 1)
    h[:, H_ONE:H_ONE + P] = 1.0
    h[:, H_I128:H_I128 + P] = np.arange(P)
    h[:, H_INS:H_INS + NS] = np.arange(NS)
    return c, h


def kernel(**inputs):
    import concourse.bacc as bacc
    from concourse.bass_utils import run_bass_kernel_spmd

    a = {k: np.asarray(v) for k, v in inputs.items()}
    w13 = np.concatenate([a["L0_ffn_w1_routed"], a["L0_ffn_w3_routed"]], axis=2)
    w13r = np.ascontiguousarray(w13.reshape(NE, DC, P, 2 * H).transpose(0, 2, 1, 3)).reshape(NE, P, W13)
    w2r = np.ascontiguousarray(a["L0_ffn_w2_routed"].reshape(NE, 2, HC, D).transpose(0, 2, 1, 3)).reshape(NE, HC, W2C)
    w13s = np.concatenate([a["L0_ffn_w1_shared"], a["L0_ffn_w3_shared"], a["L0_ffn_gate_w"].T], axis=1)
    w13s = np.ascontiguousarray(w13s.reshape(DC, P, GS).transpose(1, 0, 2)).reshape(P, DC * GS)
    w2s = np.ascontiguousarray(a["L0_ffn_w2_shared"].reshape(2, HC, D).transpose(1, 0, 2)).reshape(HC, W2C)
    hd = D // HEADS
    wm = [a["L0_attn_W_in"].T, np.repeat(a["L0_attn_W_dt"], hd, axis=0).T, a["L0_attn_W_out"].T]
    wm = np.concatenate([w.reshape(DC, P, D).transpose(1, 0, 2).reshape(P, DC * D) for w in wm], axis=1)
    cst, hcst = _constants()
    cst[:, C_GB:C_GB + NE] = a["L0_ffn_gate_b"][None, :]
    cst[:, C_MB:C_MB + DC] = a["L0_attn_log_A"].reshape(DC, P).T
    cst[:, C_MB + DC:C_MB + 2 * DC] = np.repeat(a["L0_attn_b_dt"], hd).reshape(DC, P).T
    arrays = {
        "x_in": a["L0_attn_x"].reshape(N, D), "w13r": w13r, "w2r": w2r, "w13s": w13s, "w2s": w2s,
        "wm": wm, "cst": cst, "hcst": hcst,
    }
    arrays = {"in_" + k: np.ascontiguousarray(v) for k, v in arrays.items()}
    nc = bacc.Bacc("TRN2", target_bir_lowering=False, num_devices=1)
    args = [nc.dram_tensor(k, v.shape, mybir.dt.from_np(v.dtype), kind="ExternalInput").ap()
            for k, v in arrays.items()]
    out = nc.dram_tensor("out", (N, D), mybir.dt.float32, kind="ExternalOutput").ap()
    build(nc, *args, out)
    r = run_bass_kernel_spmd(nc, [arrays], core_ids=[0])
    return r.results[0]["out"].reshape(B, T, D)
```

```python
import concourse.bass as bass
from concourse import mybir
from contextlib import ExitStack
import numpy as np

B, T, D = 4, 512, 256
H = 176
NE, TOPK = 16, 4
HEADS = 32
P = 128
N = B * T
NT = N // P
DC = D // P
HC = H // 2
NSLOT_MAX = (N * TOPK + NE * (P - 1)) // P
UN = 4
NS = -(-NSLOT_MAX // UN) * UN
STEPS = NT + NS
LAG_X, LAG_H, LAG_T, LAG_Y = 0, 2, 3, 5
LAG_E = 1
LAGS = (LAG_X, LAG_H, LAG_T, LAG_Y)
EPS = 1e-5
W13 = DC * 2 * H
W2C = 2 * D
WE = W13 + W2C
GS = 2 * H + NE
WSH = DC * GS + W2C
MCH = 256
NMC = N // MCH
MT = MCH // P
M_LAG = 4
MAMBA_E = 12
MW = 3 * DC * D

C_ID, C_TOK, C_IE, C_J128, C_ONE, C_GB, C_MB = 0, 128, 144, 160, 176, 177, 193
NCST = C_MB + 4
H_TRI, H_ONE, H_I128, H_INS = 0, 128, 256, 384
NHCST = 384 + NS


def build(nc, x_d, w13r_d, w2r_d, w13s_d, w2s_d, wm_d, cst_d, hcst_d, out_d):
    f32, f32r, f16, i32, u32 = (mybir.dt.float32, mybir.dt.float32r, mybir.dt.float16,
                                mybir.dt.int32, mybir.dt.uint32)
    ALU = mybir.AluOpType
    ACT = mybir.ActivationFunctionType
    AX = mybir.AxisListType
    ds = bass.ds
    ctx = ExitStack()
    with ctx:
        def sb(name, shape, dt=f32):
            return ctx.enter_context(nc.sbuf_tensor(name, shape, dt))

        def sem(name):
            return ctx.enter_context(nc.semaphore(name))

        xn_dram = nc.dram_tensor("xn_scratch", (N, D), f32, kind="Internal").ap()
        ys_dram = nc.dram_tensor("ys_scratch", (NS * P, D), f32, kind="Internal").ap()

        w_routed = sb("w_routed", [P, NE, 2, WE], f32r)
        w_shared = sb("w_shared", [P, 2, WSH], f32r)
        stage = [sb("stage0", [P, WSH]), sb("stage1", [P, WE])]
        xres = sb("xres", [P, NT, D])
        ring_r = sb("ring_r", [P, 2048], f32r)
        ring_f = sb("ring_f", [P, 2048])
        xT = [[ring_r[:, (b * 2 + h) * 256:(b * 2 + h + 1) * 256] for h in range(2)] for b in range(2)]
        hT = [[ring_r[:, 1024 + (b * 2 + h) * 256:1024 + (b * 2 + h + 1) * 256] for h in range(2)] for b in range(2)]
        xg = [ring_f[:, k * D:(k + 1) * D] for k in range(UN)]
        hid = [ring_f[:, 1024 + b * H:1024 + (b + 1) * H] for b in range(2)]
        yb = [ring_f[:, 1376 + b * D:1376 + (b + 1) * D] for b in range(2)]
        oh = ring_f[:, 0:1024].rearrange("p (t k e) -> p t k e", t=NT, k=TOPK)
        prod = ring_f[:, 1024:2048].rearrange("p (t k e) -> p t k e", t=NT, k=TOPK)
        ring_h = ring_f[:, :].bitcast(f16)
        pickA = [ring_h[:, b * 512:(b + 1) * 512].rearrange("p (k s) -> p k s", k=TOPK) for b in range(2)]
        pickB = [ring_h[:, 1024 + b * TOPK * NS:1024 + (b + 1) * TOPK * NS].rearrange("p (k s) -> p k s", k=TOPK)
                 for b in range(2)]
        teq = ring_f[0:1, 0:NS * NE].rearrange("p (j e) -> p j e", e=NE)
        cst = sb("cst", [P, NCST])
        hcst = sb("hcst", [P, NHCST], f16)
        ident = cst[:, C_ID:C_ID + P]
        lg = sb("lg", [P, NT, NE])
        lg_room = lg[:, :, :].rearrange("p t e -> p (t e)")
        stats = lg_room[:, 0:NT * 6].rearrange("p (t s) -> p t s", s=6)
        mv = lg_room[:, NT * 6:NT * 8].rearrange("p (t s) -> p t s", s=2)
        veps = lg_room[:, NT * 8:NT * 9]
        ntmp = lg_room[:, NT * 9:NT * 10]
        rstd = sb("rstd", [P, NT])
        nmr = sb("nmr", [P, NT])
        rt = [stage[0], stage[1]]
        si = sb("si", [P, NT * TOPK], i32)
        wk = sb("wk", [P, NT * TOPK])
        te = sb("te", [1, NS], i32)
        tokidx = sb("tokidx", [P, NS], i32)
        nega = sb("nega", [P, DC])
        r0 = lambda a, b: rt[0][:, a:b]
        r1 = lambda a, b: rt[1][:, a:b]
        v8 = r0(0, 128).rearrange("p (t k) -> p t k", k=8)
        i8 = r0(128, 256).bitcast(u32).rearrange("p (t k) -> p t k", k=8)
        if4 = r0(256, 320)
        wsum = r0(320, 336)
        rw = r0(336, 352)
        slotf = r0(352, 416)
        loi = r0(416, 480).bitcast(i32)
        hii = r0(480, 544).bitcast(i32)
        lof = r0(544, 608)
        hif = r0(608, 672)
        memh = r0(672, 800).bitcast(f16)
        totT = r0(800, 1056)
        gsum = r1(0, 256)
        gexc = r1(256, 512)
        slot = r1(512, 768)
        cmpj = r1(768, 1024)
        cnt = r1(1024, 1040)
        ntl = r1(1040, 1056)
        ctl = r1(1056, 1072)
        tbx = r1(1072, 1088)
        off = r1(1088, 1104)
        tef = r1(1104, 1104 + NS)

        mroom = w_routed[:, MAMBA_E:NE, :, :].rearrange("p e h w -> p (e h w)")
        m_w = [mroom[:, h * MW:(h + 1) * MW] for h in range(2)]
        mo = 2 * MW
        m_xT = [[mroom[:, mo + (b * 2 + h) * 512:mo + (b * 2 + h + 1) * 512] for h in range(2)] for b in range(2)]
        m_xp = [ring_r[:, h * 512:(h + 1) * 512] for h in range(2)]
        m_ys = [ring_r[:, 1024 + h * 512:1024 + (h + 1) * 512] for h in range(2)]
        co = mo + 2048
        cg = [mroom[:, co + b * 1024:co + (b + 1) * 1024].bitcast(f32).rearrange("p (k d) -> p k d", k=TOPK)
              for b in range(4)]
        m_t = [ring_f[:, b * 512:(b + 1) * 512] for b in range(2)]
        m_r = [ring_f[:, 1024 + b * 512:1024 + (b + 1) * 512] for b in range(2)]
        m_xn = [stage[b][:, 0:512].rearrange("p (t d) -> p t d", t=MT) for b in range(2)]
        m_y = [stage[b][:, 512:1024] for b in range(2)]

        pb = [ctx.enter_context(nc.psum_tensor(f"bank{i}", [P, 512], f32)) for i in range(8)]
        q_xT, q_xp, q_z, q_y = pb[0:2], pb[2:5], pb[5:7], pb[7]
        p_xT, p_h, p_hT, p_y = pb[0:2], pb[2:4], pb[4:6], pb[6:8]

        s_cst = sem("constants_loaded")
        s_x = [sem(f"x_loaded{i}") for i in range(4)]
        s_stg = [sem(f"stage_loaded{i}") for i in range(2)]
        s_whi = sem("weights_high")
        s_wla = sem("weights_low_up")
        s_wlo = sem("weights_low_down")
        s_ln = sem("variances_ready")
        s_sd = sem("deviation_ready")
        s_xn = sem("xn_ready")
        s_xw = [sem(f"xn_written{k}") for k in range(UN)]
        s_g = [sem(f"gathered{k}") for k in range(UN)]
        s_xt = sem("x_transposed")
        s_xhi = sem("xT_high")
        s_xlo = sem("xT_low")
        s_h = sem("hidden_sums")
        s_lg = sem("logits_copied")
        s_a = sem("hidden_first")
        s_m = sem("hidden_product")
        s_s = sem("hidden_silu")
        s_ht = sem("hidden_transposed")
        s_hhi = sem("hT_high")
        s_hlo = sem("hT_low")
        s_y = sem("y_sums")
        s_yo = sem("y_out")
        s_yw = [sem(f"y_written{b}") for b in range(2)]
        s_sig = sem("sigmoid_ready")
        s_mem = sem("members_ready")
        s_cum = sem("counts_ready")
        s_pk = sem("picks_ready")
        s_pkd = sem("picks_used")
        s_rt = sem("routing_ready")
        s_cg = [sem(f"combine_gathered{b}") for b in range(4)]
        s_cd = sem("combined")
        s_dv = sem("dve_chain")
        s_fin = sem("layer_done")
        s_out = sem("out_written")
        m_s = {n: sem("m_" + n) for n in ("var", "ln", "r0", "scale", "xn", "xt", "xhi", "xlo", "xp", "phi", "plo", "z",
                                          "abs", "relu", "exp", "log", "sp", "a", "scan", "yhi", "ylo", "y", "res",
                                          "neg")}

        def term(f, t, q):
            return f * NT * TOPK + (t // 2) * 2 * TOPK + 2 * q + t % 2 + 1

        def staggered(stages):
            for s in range(NMC + M_LAG):
                for lag, stage_of in stages:
                    if 0 <= s - lag < NMC:
                        stage_of(s - lag)

        block = ctx.enter_context(nc.Block())

        def pipeline(eng, count, stages):
            depth = max(LAGS) + 2
            bodies = (count - depth) // UN

            def step(i, c):
                for lag, stage in stages:
                    if isinstance(i, int) and not 0 <= i * UN + c - lag < count:
                        continue
                    stage(i, c - lag)

            for c in range(depth):
                step(0, c)
            with eng.Fori(0, bodies) as i:
                for c in range(depth, depth + UN):
                    step(i, c)
            for c in range(depth + bodies * UN, count + max(LAGS)):
                step(0, c)

        def item_parts(i, e=None):
            if i == "shared":
                return [(P, slice(0, DC * GS), lambda h: w_shared[:, h, 0:DC * GS]),
                        (HC, slice(DC * GS, WSH), lambda h: w_shared[0:HC, h, DC * GS:WSH])]
            if i == "routed":
                return [(P, slice(0, W13), lambda h: w_routed[:, ds(e, 1), h, 0:W13]),
                        (HC, slice(W13, WE), lambda h: w_routed[0:HC, ds(e, 1), h, W13:WE])]
            if i == "m1":
                return [(P, slice(0, 512), lambda h: m_w[h][:, 0:512]),
                        (P, slice(512, 1024), lambda h: m_w[h][:, 512:1024])]
            return [(P, slice(0, 256), lambda h: m_w[h][:, 1024:1280]),
                    (P, slice(256, 512), lambda h: m_w[h][:, 1280:MW])]

        ITEM_M = 17
        ITEM_AGAIN = 19

        @block.sync
        def _(sp):
            sp.dma_start(cst[:, :], cst_d).then_inc(s_cst, 16)
            x_v = x_d.rearrange("(t p) d -> p t d", p=P)
            for q in range(4):
                sp.dma_start(xres[:, 4 * q:4 * q + 4, :], x_v[:, 4 * q:4 * q + 4, :]).then_inc(s_x[q], 16)

            def load(b, wait, a_src, a_cols, b_src=None, b_cols=None):
                if wait is not None:
                    sp.wait_ge(s_wlo, wait)
                    sp.wait_ge(s_wla, wait)
                sp.dma_start(stage[b][:, 0:a_cols], a_src).then_inc(s_stg[b], 16)
                if b_src is not None:
                    sp.dma_start(stage[b][0:HC, a_cols:b_cols], b_src).then_inc(s_stg[b], 16)

            def load_expert(b, wait, e):
                load(b, wait, w13r_d[ds(e, 1), :, :].rearrange("o p c -> (o p) c"), W13,
                     w2r_d[ds(e, 1), :, :].rearrange("o p c -> (o p) c"), WE)

            def xn_out(f, i, c):
                t = i * UN + c
                sp.wait_ge(s_xn, f * NT + t + 1)
                sp.dma_start(xn_dram[ds(t * P, P), :], xg[c % UN]).then_inc(s_xw[c % UN], 16)

            def y_out(f, i, c):
                j = i * UN + c
                sp.wait_ge(s_yo, f * STEPS + NT + j + 1)
                sp.dma_start(ys_dram[ds(j * P, P), :], yb[c % 2]).then_inc(s_yw[c % 2], 16)

            load(0, None, w13s_d, DC * GS, w2s_d, WSH)
            sp.dma_start(hcst[:, :], hcst_d).then_inc(s_cst, 16)
            load_expert(1, None, 0)
            for f in range(2):
                if f == 0:
                    for t in range(2):
                        xn_out(f, 0, t)
                        load_expert(t % 2, t + 1, t + 1)
                    with sp.Fori(0, (NT - UN) // UN) as i:
                        for c in range(2, 2 + UN):
                            xn_out(f, i, c)
                            load_expert(c % 2, i * UN + c + 1, i * UN + c + 1)
                    for t in range(NT - 2, NT):
                        xn_out(f, 0, t)
                        if t + 1 < NE:
                            load_expert(t % 2, t + 1, t + 1)
                else:
                    sp.wait_ge(m_s["res"], NMC)
                    for t in range(2):
                        load_expert((ITEM_AGAIN + t) % 2, ITEM_AGAIN + t - 1, MAMBA_E + t)
                    with sp.Fori(0, NT // UN) as i:
                        for k in range(UN):
                            xn_out(f, i, k)
                    for t in range(2, NE - MAMBA_E):
                        load_expert((ITEM_AGAIN + t) % 2, ITEM_AGAIN + t - 1, MAMBA_E + t)
                with sp.Fori(0, NS // UN) as i:
                    for k in range(UN):
                        y_out(f, i, k)
                if f == 0:
                    load(ITEM_M % 2, ITEM_M, wm_d[:, 0:1024], 1024)
                    load((ITEM_M + 1) % 2, ITEM_M, wm_d[:, 1024:MW], 512)
            o_v = out_d.rearrange("(t p) d -> p t d", p=P)
            with sp.Fori(0, NT // 2) as i:
                for b in range(2):
                    t = i * 2 + b
                    sp.wait_ge(s_cd, NT * TOPK + i * 2 * TOPK + 2 * (TOPK - 1) + b + 1)
                    sp.dma_start(o_v[:, ds(t, 1), :], xres[:, ds(t, 1), :]).then_inc(s_out, 16)
            sp.wait_ge(s_out, 16 * NT)

        @block.gpsimd
        def _(pool):
            def low_item(i, kind, b, e=None):
                pool.wait_ge(s_whi, i + 1)
                rows, cols, view = item_parts(kind, e)[-1]
                pool.tensor_tensor(view(1), stage[b][0:rows, cols], view(0).bitcast(f32), ALU.subtract
                                   ).then_inc(s_wlo, 1)

            def gather(f, j):
                if j >= UN:
                    pool.wait_ge(s_xt, f * STEPS + NT + j - UN + 1)
                pool.indirect_dma_start(xg[j % UN], None, xn_dram,
                                        bass.IndirectOffsetOnAxis(ap=tokidx[:, j:j + 1], axis=0)
                                        ).then_inc(s_g[j % UN], 16)

            def combine(f, t):
                if t >= 4:
                    pool.wait_ge(s_cd, term(f, t - 4, TOPK - 1))
                for q in range(TOPK):
                    n = t * TOPK + q
                    pool.indirect_dma_start(cg[t % 4][:, q, :], None, ys_dram,
                                            bass.IndirectOffsetOnAxis(ap=si[:, n:n + 1], axis=0)
                                            ).then_inc(s_cg[t % 4], 16)

            low_item(0, "shared", 0)
            for f in range(2):
                if f == 0:
                    with pool.Fori(0, NT // UN) as i:
                        for k in range(UN):
                            low_item(i * UN + k + 1, "routed", (k + 1) % 2, i * UN + k)
                else:
                    for t in range(UN):
                        low_item(ITEM_AGAIN + t, "routed", (ITEM_AGAIN + t) % 2, MAMBA_E + t)
                pool.wait_ge(s_rt, f + 1)
                for k in range(UN):
                    pool.wait_ge(s_xw[k], 16 * (NT // UN) * (f + 1))
                for j in range(NS):
                    gather(f, j)
                for b in range(2):
                    pool.wait_ge(s_yw[b], 16 * (NS // 2) * (f + 1))
                for t in range(NT):
                    combine(f, t)
                    if f == 0 and t == 0:
                        low_item(ITEM_M, "m1", ITEM_M % 2)
                        low_item(ITEM_M + 1, "m2", (ITEM_M + 1) % 2)

        @block.scalar
        def _(act):
            def high(parts, b):
                for rows, cols, view in parts:
                    last = act.activation(view(0), stage[b][0:rows, cols], ACT.Copy)
                last.then_inc(s_whi, 1)

            def high_item(b, uses, kind, dmas, e=None):
                act.wait_ge(s_stg[b], 16 * uses)
                high(item_parts(kind, e), b)

            def deviation(l):
                act.wait_ge(s_ln, l + 1)
                act.activation(rstd[:, :], rstd[:, :], ACT.Sqrt).then_inc(s_sd, 1)

            def act_x(base, early):
                def stage(i, c):
                    n, b = base + i * UN + c, c % 2
                    act.wait_ge(s_xt, n + 1)
                    if not (early and isinstance(i, int) and c < 2):
                        act.wait_ge(s_h, n - 1)
                    act.activation(xT[b][0], p_xT[b][:, 0:DC * P], ACT.Copy).then_inc(s_xhi, 1)
                return stage

            def act_ht(base, early):
                def stage(i, c):
                    n, b = base + i * UN + c, c % 2
                    act.wait_ge(s_ht, n + 1)
                    if not (early and isinstance(i, int) and c < 2):
                        act.wait_ge(s_y, n - 1)
                    act.activation(hT[b][0][0:HC, :], p_hT[b][0:HC, 0:2 * P], ACT.Copy).then_inc(s_hhi, 1)
                return stage

            def act_first(base, early, shared):
                def stage(i, c):
                    n, b = base + i * UN + c, c % 2
                    act.wait_ge(s_h, n + 1)
                    if shared:
                        act.activation(lg[:, ds(i * UN + c, 1), :], p_h[b][:, 2 * H:GS], ACT.Copy).then_inc(s_lg, 1)
                    if not (early and isinstance(i, int) and c < 2):
                        act.wait_ge(s_ht, n - 1)
                    if shared:
                        act.activation(hid[b], p_h[b][:, 0:H], ACT.Silu).then_inc(s_a, 1)
                    else:
                        act.activation(hid[b], p_h[b][:, H:2 * H], ACT.Copy).then_inc(s_a, 1)
                return stage

            def act_silu(base):
                def stage(i, c):
                    act.wait_ge(s_m, base + i * UN + c + 1)
                    act.activation(hid[c % 2], hid[c % 2], ACT.Silu).then_inc(s_s, 1)
                return stage

            def act_expert(i, c):
                high_item((c + 1) % 2, i * UN + 2 * ((c + 1) // 2) + 2, "routed", 2, i * UN + c)

            def again(first, end):
                for c in range(first, end):
                    b = (ITEM_AGAIN + c) % 2
                    high_item(b, M_BASE[b] + 2 * (c // 2 + 1), "routed", 2, MAMBA_E + c)

            act.wait_ge(s_cst, 16)
            high_item(0, 2, "shared", 2)
            deviation(0)
            for f in range(2):
                base = f * STEPS
                pipeline(act, NT, [(LAG_H, act_first(base, f == 0, True)), (LAG_X, act_x(base, f == 0)),
                                   (LAG_T, act_ht(base, f == 0))] + ([(LAG_X, act_expert)] if f == 0 else []))
                if f == 1:
                    again(2, NE - MAMBA_E)
                act.wait_ge(s_lg, NT * (f + 1))
                act.activation(lg[:, :, :], lg[:, :, :], ACT.Sigmoid).then_inc(s_sig, 1)
                base += NT
                pipeline(act, NS, [(LAG_H, act_first(base, False, False)), (LAG_X, act_x(base, False)),
                                   (LAG_H, act_silu(base)), (LAG_T, act_ht(base, False))])
                if f == 0:
                    act.wait_ge(s_y, STEPS)
                    for q, kind in ((ITEM_M, "m1"), (ITEM_M + 1, "m2")):
                        high_item(q % 2, M_FIRST[q % 2] + 1, kind, 1)
                    act.activation(nega[:, :], cst[:, C_MB:C_MB + DC], ACT.Exp).then_inc(m_s["neg"], 1)
                    act.wait_ge(m_s["neg"], 1)
                    act.activation(nega[:, :], nega[:, :], ACT.Copy, scale=-1.0).then_inc(m_s["neg"], 1)
                    act.wait_ge(m_s["neg"], 2)

                    def root(c):
                        tt = slice(c * MT, (c + 1) * MT)
                        act.wait_ge(m_s["var"], c + 1)
                        act.activation(rstd[:, tt], veps[:, tt], ACT.Ln).then_inc(m_s["ln"], 1)
                        act.wait_ge(m_s["ln"], c + 1)
                        act.activation(rstd[:, tt], rstd[:, tt], ACT.Exp, scale=-0.5).then_inc(m_s["r0"], 1)

                    def normalise(c):
                        act.wait_ge(m_s["scale"], c + 1)
                        if c < 2:
                            act.wait_ge(s_wla, ITEM_AGAIN)
                            act.wait_ge(s_wlo, ITEM_AGAIN)
                        else:
                            act.wait_ge(m_s["xt"], c - 1)
                        for q in range(MT):
                            t = c * MT + q
                            last = act.activation(m_xn[c % 2][:, q, :], xres[:, t, :], ACT.Identity,
                                                  bias=nmr[:, t:t + 1], scale=rstd[:, t:t + 1])
                        last.then_inc(m_s["xn"], 1)

                    def x_high(c):
                        act.wait_ge(m_s["xt"], c + 1)
                        if c >= 2:
                            act.wait_ge(m_s["xp"], c - 1)
                        act.activation(m_xT[c % 2][0], q_xT[c % 2][:, :], ACT.Copy).then_inc(m_s["xhi"], 1)

                    def xp_high(c):
                        act.wait_ge(m_s["xp"], c + 1)
                        if c >= 1:
                            act.wait_ge(m_s["z"], c)
                        act.activation(m_xp[0], q_xp[c % 3][:, :], ACT.Copy).then_inc(m_s["phi"], 1)

                    def logarithm(c):
                        b = c % 2
                        act.wait_ge(m_s["z"], c + 1)
                        if c >= 2:
                            act.wait_ge(m_s["scan"], c - 1)
                        for q in range(DC):
                            qs = slice(q * MCH, (q + 1) * MCH)
                            bias = cst[:, C_MB + DC + q:C_MB + DC + q + 1]
                            act.activation(m_r[b][:, qs], q_z[b][:, qs], ACT.Relu, bias=bias)
                            last = act.activation(m_t[b][:, qs], q_z[b][:, qs], ACT.Abs, bias=bias)
                        last.then_inc(m_s["abs"], 1)
                        act.wait_ge(m_s["abs"], c + 1)
                        act.activation(m_t[b], m_t[b], ACT.Exp, scale=-1.0).then_inc(m_s["exp"], 1)
                        act.wait_ge(m_s["exp"], c + 1)
                        act.activation(m_t[b], m_t[b], ACT.Ln, bias=1.0).then_inc(m_s["log"], 1)

                    def decay(c):
                        act.wait_ge(m_s["sp"], c + 1)
                        for q in range(DC):
                            qs = slice(q * MCH, (q + 1) * MCH)
                            last = act.activation(m_t[c % 2][:, qs], m_t[c % 2][:, qs], ACT.Exp,
                                                  scale=nega[:, q:q + 1])
                        last.then_inc(m_s["a"], 1)

                    def y_high(c):
                        act.wait_ge(m_s["scan"], c + 1)
                        if c >= 1:
                            act.wait_ge(m_s["y"], c)
                        act.activation(m_ys[0], m_y[c % 2], ACT.Copy).then_inc(m_s["yhi"], 1)

                    staggered([(2, xp_high), (3, decay), (1, normalise), (1, x_high), (3, y_high), (2, logarithm),
                               (0, root)])
                    deviation(1)
                    again(0, 2)

        @block.vector
        def _(dve):
            chain = [0]

            def link(ins):
                chain[0] += 1
                ins.then_inc(s_dv, 1)
                dve.wait_ge(s_dv, chain[0])

            def mark(ins):
                chain[0] += 1
                ins.then_inc(s_dv, 1)
                return chain[0]

            def statistics(t):
                return dve.bn_stats(stats[:, t, :], xres[:, t, :])

            def variances():
                for t in range(NT):
                    last = dve.bn_aggr(mv[:, t, :], stats[:, t, :])
                link(last)
                dve.tensor_scalar(rstd[:, :], mv[:, :, 1], EPS, None, ALU.add).then_inc(s_ln, 1)

            def scales(l):
                dve.wait_ge(s_sd, l + 1)
                link(dve.reciprocal(rstd[:, :], rstd[:, :]))
                link(dve.scalar_tensor_tensor(nmr[:, :], mv[:, :, 0], -1.0, rstd[:, :], ALU.mult, ALU.mult))

            def dve_norm(f):
                def stage(i, c):
                    t = i * UN + c
                    if not (isinstance(i, int) and c < UN):
                        dve.wait_ge(s_xt, f * STEPS + t - UN + 1)
                        dve.wait_ge(s_xw[c % UN], 16 * (f * (NT // UN) + i + c // UN))
                    dve.tensor_scalar(xg[c % UN], xres[:, ds(t, 1), :].rearrange("p o d -> p (o d)"),
                                      rstd[:, ds(t, 1)], nmr[:, ds(t, 1)], ALU.mult, ALU.add).then_inc(s_xn, 1)
                return stage

            def dve_x(base):
                def stage(i, c):
                    b = c % 2
                    dve.wait_ge(s_xhi, base + i * UN + c + 1)
                    dve.tensor_tensor(xT[b][1], p_xT[b][:, 0:DC * P], xT[b][0].bitcast(f32),
                                      ALU.subtract).then_inc(s_xlo, 1)
                return stage

            def dve_ht(base):
                def stage(i, c):
                    b = c % 2
                    dve.wait_ge(s_hhi, base + i * UN + c + 1)
                    dve.tensor_tensor(hT[b][1][0:HC, :], p_hT[b][0:HC, 0:2 * P], hT[b][0][0:HC, :].bitcast(f32),
                                      ALU.subtract).then_inc(s_hlo, 1)
                return stage

            def dve_product(base, shared):
                def stage(i, c):
                    b = c % 2
                    dve.wait_ge(s_a, base + i * UN + c + 1)
                    cols = slice(H, 2 * H) if shared else slice(0, H)
                    dve.tensor_tensor(hid[b], p_h[b][:, cols], hid[b], ALU.mult).then_inc(s_m, 1)
                return stage

            def dve_shared_out(base):
                def stage(i, c):
                    dve.wait_ge(s_y, base + i * UN + c + 1)
                    xr = xres[:, ds(i * UN + c, 1), :].rearrange("p o d -> p (o d)")
                    dve.scalar_tensor_tensor(xr, p_y[c % 2][:, 0:D], 0.5, xr, ALU.mult, ALU.add).then_inc(s_yo, 1)
                return stage

            def dve_slot_out(f, base):
                def stage(i, c):
                    b = c % 2
                    dve.wait_ge(s_y, base + i * UN + c + 1)
                    if not (isinstance(i, int) and i * UN + c < 2):
                        dve.wait_ge(s_yw[b], 16 * (f * (NS // 2) + i * (UN // 2) + c // 2))
                    dve.tensor_copy(yb[b], p_y[b][:, 0:D]).then_inc(s_yo, 1)
                return stage

            def dve_expert(i, c):
                dve.wait_ge(s_whi, i * UN + c + 2)
                low_up("routed", (c + 1) % 2, i * UN + c)

            def low_up(kind, b, e=None):
                rows, cols, view = item_parts(kind, e)[0]
                dve.tensor_tensor(view(1), stage[b][0:rows, cols], view(0).bitcast(f32), ALU.subtract
                                  ).then_inc(s_wla, 1)

            def route(f):
                dve.wait_ge(s_sig, f + 1)
                dve.wait_ge(s_wlo, ITEM_M if f == 0 else ITEM_AGAIN + NE - MAMBA_E)
                link(dve.tensor_tensor(lg[:, :, :], lg[:, :, :],
                                       cst[:, C_GB:C_GB + NE].unsqueeze(1).broadcast_to((P, NT, NE)), ALU.add))
                for t in range(NT):
                    last = dve.max(v8[:, t, :], lg[:, t, :])
                link(last)
                for t in range(NT):
                    last = dve.max_index(i8[:, t, :], v8[:, t, :], lg[:, t, :])
                link(last)
                v4 = v8[:, :, 0:TOPK]
                if4v = if4.rearrange("p (t k) -> p t k", k=TOPK)
                link(dve.tensor_copy(if4v, i8[:, :, 0:TOPK]))
                for k in range(UN):
                    dve.wait_ge(s_xw[k], 16 * (NT // UN) * (f + 1))
                ie = cst[:, C_IE:C_IE + NE]
                link(dve.tensor_tensor(oh.rearrange("p t k e -> p (t k) e"),
                                       if4.unsqueeze(2).broadcast_to((P, NT * TOPK, NE)),
                                       ie.unsqueeze(1).broadcast_to((P, NT * TOPK, NE)), ALU.is_equal))
                dve.tensor_reduce(prod.rearrange("p t k e -> p (t k e)")[:, 0:NT * NE].rearrange(
                    "p (t e) -> p t e", e=NE), oh.rearrange("p t k e -> p t e k"), AX.X, ALU.add
                    ).then_inc(s_dv, 1)
                chain[0] += 1
                dve.wait_ge(s_dv, chain[0])
                dve.tensor_copy(memh, prod.rearrange("p t k e -> p (t k e)")[:, 0:NT * NE]).then_inc(s_mem, 1)
                link(dve.tensor_reduce(wsum, v4, AX.X, ALU.add))
                link(dve.reciprocal(rw, wsum))
                link(dve.tensor_scalar(rw, rw, 0.5, None, ALU.mult))
                link(dve.tensor_tensor(wk[:, :].rearrange("p (t k) -> p t k", k=TOPK), v4,
                                       rw.unsqueeze(2).broadcast_to((P, NT, TOPK)), ALU.mult))
                dve.wait_ge(s_cum, f + 1)
                totTv = totT.rearrange("p (e t) -> p e t", e=NE)
                link(dve.tensor_copy(totTv, pb[1][:, 0:NT * NE].rearrange("p (t e) -> p e t", e=NE)))
                one = cst[:, C_ONE:C_ONE + 1]
                link(dve.tensor_tensor_scan(gsum, one.broadcast_to((P, NT * NE)), totT, 0.0, ALU.mult, ALU.add))
                link(dve.tensor_tensor(gexc, gsum, totT, ALU.subtract))
                gs3 = gsum.rearrange("p (e t) -> p e t", e=NE)
                ge3 = gexc.rearrange("p (e t) -> p e t", e=NE)
                link(dve.tensor_tensor(cnt, gs3[:, :, NT - 1], ge3[:, :, 0], ALU.subtract))
                cj = cmpj.rearrange("p (e j) -> p e j", e=NE)
                link(dve.tensor_tensor(cj, cnt.unsqueeze(2).broadcast_to((P, NE, 16)),
                                       cst[:, C_J128:C_J128 + 16].unsqueeze(1).broadcast_to((P, NE, 16)), ALU.is_gt))
                link(dve.tensor_reduce(ntl, cj, AX.X, ALU.add))
                link(dve.tensor_tensor_scan(ctl, one.broadcast_to((P, NE)), ntl, 0.0, ALU.mult, ALU.add))
                link(dve.tensor_tensor(tbx, ctl, ntl, ALU.subtract))
                link(dve.scalar_tensor_tensor(off, tbx, float(P), ge3[:, :, 0], ALU.mult, ALU.subtract))
                sl = slot.rearrange("p (t e) -> p t e", e=NE)
                link(dve.tensor_tensor(sl, pb[0][:, 0:NT * NE].rearrange("p (t e) -> p t e", e=NE),
                                       gexc.rearrange("p (e t) -> p t e", e=NE), ALU.add))
                link(dve.tensor_tensor(sl, sl, off.unsqueeze(1).broadcast_to((P, NT, NE)), ALU.add))
                for k in range(TOPK):
                    last = dve.tensor_tensor(prod[:, :, k, :], oh[:, :, k, :], sl, ALU.mult)
                link(last)
                link(dve.tensor_reduce(slotf, prod.rearrange("p t k e -> p (t k) e"), AX.X, ALU.add))
                link(dve.tensor_copy(si[:, :], slotf))
                dve.tensor_single_scalar(loi, si[:, :], P - 1, ALU.bitwise_and)
                link(dve.tensor_single_scalar(hii, si[:, :], 7, ALU.logical_shift_right))
                dve.tensor_copy(lof, loi)
                link(dve.tensor_copy(hif, hii))
                for t in range(NT):
                    if t >= 2:
                        dve.wait_ge(s_pkd, f * NT + t - 1)
                    dve.tensor_tensor(pickA[t % 2], hcst[:, H_I128:H_I128 + P].unsqueeze(1).broadcast_to((P, TOPK, P)),
                                      lof[:, t * TOPK:(t + 1) * TOPK].unsqueeze(2).broadcast_to((P, TOPK, P)),
                                      ALU.is_equal)
                    for k in range(TOPK):
                        q = t * TOPK + k
                        last = dve.tensor_scalar(pickB[t % 2][:, k, :], hcst[:, H_INS:H_INS + NS], hif[:, q:q + 1],
                                                 cst[:, C_TOK + t:C_TOK + t + 1], ALU.is_equal, ALU.mult)
                    last.then_inc(s_pk, 1)
                dve.wait_ge(s_pkd, (f + 1) * NT)
                link(dve.tensor_tensor(teq, hcst[0:1, H_INS:H_INS + NS].unsqueeze(2).broadcast_to((1, NS, NE)),
                                       ctl[0:1, :].unsqueeze(1).broadcast_to((1, NS, NE)), ALU.is_ge))
                link(dve.tensor_reduce(tef[0:1, :], teq, AX.X, ALU.add))
                link(dve.tensor_scalar(te[:, :], tef[0:1, :], float(NE - 1), None, ALU.min))
                dve.tensor_copy(tokidx[:, :], pb[2][:, 0:NS]).then_inc(s_rt, 1)

            def combine(f, i, c):
                for q in range(TOPK):
                    for b in range(2):
                        t = i * 4 + 2 * c + b
                        if q == 0:
                            dve.wait_ge(s_cg[2 * c + b], 16 * TOPK * (f * (NT // 4) + i + 1))
                        else:
                            dve.wait_ge(s_cd, f * NT * TOPK + (i * 2 + c) * 2 * TOPK + 2 * (q - 1) + b + 1)
                        xr = xres[:, ds(t, 1), :].rearrange("p o d -> p (o d)")
                        dve.scalar_tensor_tensor(xr, cg[2 * c + b][:, q, :], wk[:, ds(t * TOPK + q, 1)], xr,
                                                 ALU.mult, ALU.add).then_inc(s_cd, 1)

            def again(first, end):
                for c in range(first, end):
                    dve.wait_ge(s_whi, ITEM_AGAIN + c + 1)
                    low_up("routed", (ITEM_AGAIN + c) % 2, MAMBA_E + c)

            for q in range(4):
                dve.wait_ge(s_x[q], 16)
            dve.wait_ge(s_cst, 32)
            dve.wait_ge(s_whi, 1)
            low_up("shared", 0)
            for t in range(NT):
                last = statistics(t)
            link(last)
            variances()
            scales(0)
            for f in range(2):
                base = f * STEPS
                pipeline(dve, NT, [(LAG_X, dve_norm(f)), (LAG_H, dve_product(base, True)), (LAG_X, dve_x(base)),
                                   (LAG_Y, dve_shared_out(base)), (LAG_T, dve_ht(base))]
                         + ([(LAG_X, dve_expert)] if f == 0 else []))
                if f == 1:
                    again(2, NE - MAMBA_E)
                route(f)
                base += NT
                pipeline(dve, NS, [(LAG_H, dve_product(base, False)), (LAG_X, dve_x(base)),
                                   (LAG_Y, dve_slot_out(f, base)), (LAG_T, dve_ht(base))])
                if f == 1:
                    with dve.Fori(0, NT // 4) as i:
                        for c in range(2):
                            combine(f, i, c)
                else:
                    newton = [0]

                    def combined(c):
                        combine(0, c // 2, c % 2)
                        dve.wait_ge(s_cd, term(0, c * MT + 1, TOPK - 1))
                        for t in range(c * MT, (c + 1) * MT):
                            last = statistics(t)
                        link(last)
                        for t in range(c * MT, (c + 1) * MT):
                            last = dve.bn_aggr(mv[:, t, :], stats[:, t, :])
                        link(last)
                        tt = slice(c * MT, (c + 1) * MT)
                        dve.tensor_scalar(veps[:, tt], mv[:, tt, 1], EPS, None, ALU.add).then_inc(m_s["var"], 1)

                    def newton_step(n):
                        def stage_of(c):
                            tt = slice(c * MT, (c + 1) * MT)
                            r, v, w = rstd[:, tt], veps[:, tt], ntmp[:, tt]
                            if n == 0:
                                dve.wait_ge(m_s["r0"], c + 1)
                                dve.wait_ge(m_s["var"], c + 1)
                                newton[0] = mark(dve.tensor_tensor(w, r, r, ALU.mult))
                                return
                            dve.wait_ge(s_dv, newton[0])
                            if n == 1:
                                newton[0] = mark(dve.tensor_tensor(w, w, v, ALU.mult))
                            elif n == 2:
                                newton[0] = mark(dve.tensor_scalar(w, w, -0.5, 1.5, ALU.mult, ALU.add))
                            elif n == 3:
                                newton[0] = mark(dve.tensor_tensor(r, r, w, ALU.mult))
                            else:
                                dve.scalar_tensor_tensor(nmr[:, tt], mv[:, tt, 0], -1.0, r, ALU.mult, ALU.mult
                                                         ).then_inc(m_s["scale"], 1)
                        return stage_of

                    def x_low(c):
                        dve.wait_ge(m_s["xhi"], c + 1)
                        dve.tensor_tensor(m_xT[c % 2][1], q_xT[c % 2][:, :], m_xT[c % 2][0].bitcast(f32),
                                          ALU.subtract).then_inc(m_s["xlo"], 1)

                    def xp_low(c):
                        dve.wait_ge(m_s["phi"], c + 1)
                        dve.tensor_tensor(m_xp[1], q_xp[c % 3][:, :], m_xp[0].bitcast(f32), ALU.subtract
                                          ).then_inc(m_s["plo"], 1)

                    def softplus(c):
                        dve.wait_ge(m_s["log"], c + 1)
                        dve.tensor_tensor(m_t[c % 2], m_t[c % 2], m_r[c % 2], ALU.add).then_inc(m_s["sp"], 1)

                    def scan(c):
                        dve.wait_ge(m_s["a"], c + 1)
                        if c >= 2:
                            dve.wait_ge(m_s["ylo"], c - 1)
                        if c % (T // MCH):
                            dve.wait_ge(m_s["scan"], c)
                        for q in range(DC):
                            qs = slice(q * MCH, (q + 1) * MCH)
                            first = m_y[(c - 1) % 2][:, (q + 1) * MCH - 1:(q + 1) * MCH]
                            last = dve.tensor_tensor_scan(m_y[c % 2][:, qs], m_t[c % 2][:, qs], q_xp[c % 3][:, qs],
                                                          first if c % (T // MCH) else 0.0, ALU.mult, ALU.add)
                        last.then_inc(m_s["scan"], 1)

                    def y_low(c):
                        dve.wait_ge(m_s["yhi"], c + 1)
                        dve.tensor_tensor(m_ys[1], m_y[c % 2], m_ys[0].bitcast(f32), ALU.subtract
                                          ).then_inc(m_s["ylo"], 1)

                    def residual(c):
                        dve.wait_ge(m_s["y"], c + 1)
                        xr = xres[:, c * MT:(c + 1) * MT, :]
                        dve.tensor_tensor(xr, xr, q_y[:, :].rearrange("p (t d) -> p t d", t=MT), ALU.add
                                          ).then_inc(m_s["res"], 1)

                    def next_statistics(c):
                        dve.wait_ge(m_s["res"], c + 1)
                        for t in range(c * MT, (c + 1) * MT):
                            last = statistics(t)
                        if c == NMC - 1:
                            link(last)

                    for q, kind in ((ITEM_M, "m1"), (ITEM_M + 1, "m2")):
                        dve.wait_ge(s_whi, q + 1)
                        low_up(kind, q % 2)
                    staggered([(1, newton_step(0)), (2, xp_low), (1, newton_step(1)), (3, softplus),
                               (1, newton_step(2)), (4, residual), (1, newton_step(3)), (1, newton_step(4)),
                               (3, scan), (1, x_low), (3, y_low), (0, combined), (4, next_statistics)])
                    variances()
                    scales(1)
                    again(0, 2)

        @block.tensor
        def _(pe):
            def mm3(out, pairs):
                terms = [(a, b) for (a0, a1, b0, b1) in pairs for a, b in ((a0, b0), (a0, b1), (a1, b0))]
                for q, (a, b) in enumerate(terms):
                    last = pe.matmul(out, a, b, start=(q == 0), stop=(q == len(terms) - 1))
                return last

            def pe_x(base, early, ready):
                def stage(i, c):
                    b, k = c % 2, c % UN
                    ready(i, c)
                    if not (early and isinstance(i, int) and c < 2):
                        pe.wait_ge(s_xlo, base + i * UN + c - 1)
                    for q in range(DC):
                        last = pe.transpose(p_xT[b][:, q * P:(q + 1) * P], xg[k][:, q * P:(q + 1) * P], ident)
                    last.then_inc(s_xt, 1)
                return stage

            def pe_ht(base, early, ready):
                def stage(i, c):
                    b = c % 2
                    ready(i, c)
                    if not (early and isinstance(i, int) and c < 2):
                        pe.wait_ge(s_hlo, base + i * UN + c - 1)
                    for q in range(2):
                        last = pe.transpose(p_hT[b][0:HC, q * P:(q + 1) * P], hid[b][:, q * HC:(q + 1) * HC], ident)
                    last.then_inc(s_ht, 1)
                return stage

            def pe_hidden(base, early, weights, cols):
                def stage(i, c):
                    n, b = base + i * UN + c, c % 2
                    w = weights(i, c)
                    pe.wait_ge(s_xlo, n + 1)
                    if not (early and isinstance(i, int) and c < 2):
                        pe.wait_ge(s_m, n - 1)
                    mm3(p_h[b][:, 0:cols], [(xT[b][0][:, q * P:(q + 1) * P], xT[b][1][:, q * P:(q + 1) * P],
                                             w(P, 0, q * cols, cols), w(P, 1, q * cols, cols)) for q in range(DC)]
                        ).then_inc(s_h, 1)
                return stage

            def pe_out(base, early, weights, w0):
                def stage(i, c):
                    n, b = base + i * UN + c, c % 2
                    w = weights(i, c)
                    pe.wait_ge(s_hlo, n + 1)
                    if not (early and isinstance(i, int) and c < 2):
                        pe.wait_ge(s_yo, n - 1)
                    mm3(p_y[b][:, 0:D], [(hT[b][0][0:HC, q * P:(q + 1) * P], hT[b][1][0:HC, q * P:(q + 1) * P],
                                          w(HC, 0, w0 + q * D, D), w(HC, 1, w0 + q * D, D)) for q in range(2)]
                        ).then_inc(s_y, 1)
                return stage

            def shared_weights(i, c):
                return lambda rows, h, a, m: w_shared[0:rows, h, a:a + m]

            e_reg = [pe.alloc_register(f"expert{k}") for k in range(UN)]

            def load_slot_expert(i, c):
                pe.reg_load(e_reg[c % UN], te[0:1, ds(i * UN + c, 1)])

            def routed_weights(i, c):
                e = pe.snap(e_reg[c % UN], min_val=0, max_val=NE - 1)
                return lambda rows, h, a, m: w_routed[0:rows, ds(e, 1), h, a:a + m]

            pe.wait_ge(s_cst, 32)
            pe.wait_ge(s_wlo, 1)
            pe.wait_ge(s_wla, 1)
            for f in range(2):
                base = f * STEPS
                pipeline(pe, NT, [
                    (LAG_H, pe_hidden(base, f == 0, shared_weights, GS)),
                    (LAG_X, pe_x(base, f == 0, lambda i, c: pe.wait_ge(s_xn, f * NT + i * UN + c + 1))),
                    (LAG_Y, pe_out(base, f == 0, shared_weights, DC * GS)),
                    (LAG_T, pe_ht(base, f == 0, lambda i, c: pe.wait_ge(s_m, base + i * UN + c + 1)))])
                pe.wait_ge(s_mem, f + 1)
                pe.matmul(pb[0][:, 0:NT * NE], hcst[:, H_TRI:H_TRI + P], memh, start=True, stop=True)
                pe.matmul(pb[1][:, 0:NT * NE], hcst[:, H_ONE:H_ONE + P], memh, start=True, stop=True
                          ).then_inc(s_cum, 1)
                for t in range(NT):
                    pe.wait_ge(s_pk, f * NT + t + 1)
                    for k in range(TOPK):
                        last = pe.matmul(pb[2][:, 0:NS], pickA[t % 2][:, k, :], pickB[t % 2][:, k, :],
                                         start=(t == 0 and k == 0), stop=(t == NT - 1 and k == TOPK - 1))
                    last.then_inc(s_pkd, 1)
                pe.wait_ge(s_rt, f + 1)
                base += NT
                pipeline(pe, NS, [
                    (LAG_H, pe_hidden(base, False, routed_weights, 2 * H)),
                    (LAG_X, pe_x(base, False, lambda i, c: pe.wait_ge(
                        s_g[c % UN], 16 * (f * (NS // UN) + i + c // UN + 1)))),
                    (LAG_Y, pe_out(base, False, routed_weights, W13)),
                    (LAG_E, load_slot_expert),
                    (LAG_T, pe_ht(base, False, lambda i, c: pe.wait_ge(s_s, f * NS + i * UN + c + 1)))])
                if f == 0:
                    pe.wait_ge(s_wlo, ITEM_AGAIN)
                    pe.wait_ge(s_wla, ITEM_AGAIN)

                    def wc(h, m, q):
                        return m_w[h][:, (m * DC + q) * D:(m * DC + q + 1) * D]

                    def turn(c):
                        pe.wait_ge(m_s["xn"], c + 1)
                        if c >= 2:
                            pe.wait_ge(m_s["xlo"], c - 1)
                        for q in range(DC):
                            for u in range(MT):
                                last = pe.transpose(q_xT[c % 2][:, q * MCH + u * P:q * MCH + (u + 1) * P],
                                                    m_xn[c % 2][:, u, q * P:(q + 1) * P], ident)
                        last.then_inc(m_s["xt"], 1)

                    def by_channel(out, m, src):
                        for e in range(DC):
                            last = mm3(out[:, e * MCH:(e + 1) * MCH],
                                       [(wc(0, m, q)[:, e * P:(e + 1) * P], wc(1, m, q)[:, e * P:(e + 1) * P],
                                         src[0][:, q * MCH:(q + 1) * MCH], src[1][:, q * MCH:(q + 1) * MCH])
                                        for q in range(DC)])
                        return last

                    def inputs(c):
                        pe.wait_ge(m_s["xlo"], c + 1)
                        if c >= 3:
                            pe.wait_ge(m_s["scan"], c - 2)
                        by_channel(q_xp[c % 3], 0, m_xT[c % 2]).then_inc(m_s["xp"], 1)

                    def step_sizes(c):
                        pe.wait_ge(m_s["plo"], c + 1)
                        if c >= 2:
                            pe.wait_ge(m_s["abs"], c - 1)
                        by_channel(q_z[c % 2], 1, m_xp).then_inc(m_s["z"], 1)

                    def outputs(c):
                        pe.wait_ge(m_s["ylo"], c + 1)
                        if c >= 1:
                            pe.wait_ge(m_s["res"], c)
                        for u in range(MT):
                            last = mm3(q_y[:, u * D:(u + 1) * D],
                                       [(m_ys[0][:, q * MCH + u * P:q * MCH + (u + 1) * P],
                                         m_ys[1][:, q * MCH + u * P:q * MCH + (u + 1) * P],
                                         wc(0, 2, q), wc(1, 2, q)) for q in range(DC)])
                        last.then_inc(m_s["y"], 1)

                    staggered([(2, inputs), (2, step_sizes), (1, turn), (3, outputs)])


M_FIRST = [18, 16]
M_BASE = [19, 17]


def _constants():
    c = np.zeros((P, NCST), np.float32)
    c[:, C_ID:C_ID + P] = np.eye(P)
    c[:, C_TOK:C_TOK + NT] = np.arange(NT)[None, :] * P + np.arange(P)[:, None]
    c[:, C_IE:C_IE + NE] = np.arange(NE)
    c[:, C_J128:C_J128 + 16] = np.arange(16) * P
    c[:, C_ONE] = 1.0
    h = np.zeros((P, NHCST), np.float16)
    h[:, H_TRI:H_TRI + P] = np.triu(np.ones((P, P)), 1)
    h[:, H_ONE:H_ONE + P] = 1.0
    h[:, H_I128:H_I128 + P] = np.arange(P)
    h[:, H_INS:H_INS + NS] = np.arange(NS)
    return c, h


def kernel(**inputs):
    import concourse.bacc as bacc
    from concourse.bass_utils import run_bass_kernel_spmd

    a = {k: np.asarray(v) for k, v in inputs.items()}
    w13 = np.concatenate([a["L0_ffn_w1_routed"], a["L0_ffn_w3_routed"]], axis=2)
    w13r = np.ascontiguousarray(w13.reshape(NE, DC, P, 2 * H).transpose(0, 2, 1, 3)).reshape(NE, P, W13)
    w2r = np.ascontiguousarray(a["L0_ffn_w2_routed"].reshape(NE, 2, HC, D).transpose(0, 2, 1, 3)).reshape(NE, HC, W2C)
    w13s = np.concatenate([a["L0_ffn_w1_shared"], a["L0_ffn_w3_shared"], a["L0_ffn_gate_w"].T], axis=1)
    w13s = np.ascontiguousarray(w13s.reshape(DC, P, GS).transpose(1, 0, 2)).reshape(P, DC * GS)
    w2s = np.ascontiguousarray(a["L0_ffn_w2_shared"].reshape(2, HC, D).transpose(1, 0, 2)).reshape(HC, W2C)
    hd = D // HEADS
    wm = [a["L0_attn_W_in"].T, np.repeat(a["L0_attn_W_dt"], hd, axis=0).T, a["L0_attn_W_out"].T]
    wm = np.concatenate([w.reshape(DC, P, D).transpose(1, 0, 2).reshape(P, DC * D) for w in wm], axis=1)
    cst, hcst = _constants()
    cst[:, C_GB:C_GB + NE] = a["L0_ffn_gate_b"][None, :]
    cst[:, C_MB:C_MB + DC] = a["L0_attn_log_A"].reshape(DC, P).T
    cst[:, C_MB + DC:C_MB + 2 * DC] = np.repeat(a["L0_attn_b_dt"], hd).reshape(DC, P).T
    arrays = {
        "x_in": a["L0_attn_x"].reshape(N, D), "w13r": w13r, "w2r": w2r, "w13s": w13s, "w2s": w2s,
        "wm": wm, "cst": cst, "hcst": hcst,
    }
    arrays = {"in_" + k: np.ascontiguousarray(v) for k, v in arrays.items()}
    nc = bacc.Bacc("TRN2", target_bir_lowering=False, num_devices=1)
    args = [nc.dram_tensor(k, v.shape, mybir.dt.from_np(v.dtype), kind="ExternalInput").ap()
            for k, v in arrays.items()]
    out = nc.dram_tensor("out", (N, D), mybir.dt.float32, kind="ExternalOutput").ap()
    build(nc, *args, out)
    r = run_bass_kernel_spmd(nc, [arrays], core_ids=[0])
    return r.results[0]["out"].reshape(B, T, D)
```
